# Optimizing a Trainium2 kernel written in Bass

```python
import numpy as np
import jax
import jax.numpy as jnp

def _softmax(x, axis=-1):
    return jax.nn.softmax(x, axis=axis)

def _gelu(x):
    return jax.nn.gelu(x, approximate=True)

def _silu(x):
    return jax.nn.silu(x)

def _sigmoid(x):
    return jax.nn.sigmoid(x)

def _layernorm(x, axis=-1, eps=1e-05):
    m = jnp.mean(x, axis=axis, keepdims=True)
    v = jnp.var(x, axis=axis, keepdims=True)
    return (x - m) / jnp.sqrt(v + eps)

def _scatter_add(tgt, idx, src, axis=0):
    return tgt.at[idx].add(src)

def _segment_sum(src, seg, n):
    return jax.ops.segment_sum(src, seg, n)
kernel_name = 'mk_xattn_ffn_d2_seqx_r4_85f874'

def setup_inputs(seed: int=0):
    np.random.seed(seed)
    _w = jnp.asarray

    def _rec_inputs():
        import jax
        import jax.numpy as jnp
        _rk = jax.random.key(seed)
        x = 7.22e-05 + 1 * jax.random.normal(jax.random.fold_in(_rk, 1), (8, 100, 512), jnp.float32)
        _lenS = 100 - jax.random.randint(jax.random.fold_in(_rk, 7), (8,), 0, max(1, 100 // 4) + 1, jnp.int32)
        _lenS2 = 361 - jax.random.randint(jax.random.fold_in(_rk, 8), (8,), 0, max(1, 361 // 4) + 1, jnp.int32)
        _ctx_512P = jax.random.normal(jax.random.fold_in(_rk, 11), (8, 16, 128), jnp.float32)
        _ctx_512c = jax.random.dirichlet(jax.random.fold_in(_rk, 511), 0.3 * jnp.ones((16,), jnp.float32), (8, 361))
        _ctx_512t = jnp.einsum('bsk,bkd->bsd', _ctx_512c, _ctx_512P)
        _ctx_512t = _ctx_512t * jax.lax.rsqrt(jnp.mean(jnp.square(_ctx_512t)) + 1e-12) * 0.953939
        ctx_512 = -0.000514642 + 1.00011 * (_ctx_512t + 0.3 * jax.random.normal(jax.random.fold_in(_rk, 611), (8, 361, 128), jnp.float32))
        return (x, ctx_512)
    x, ctx_512 = _rec_inputs()

    def _L0_xattn_setup():
        import jax, jax.numpy as jnp
        import numpy as np
        B, S, H, NH, L = (2, 512, 512, 16, 128)
        HD = H // NH
        key = jax.random.key(seed)
        k1, k2, k3, k4, k5 = jax.random.split(key, 5)
        scale = 0.02
        return {'q': jax.random.normal(k1, (B, S, H), dtype=jnp.float32), 'latent_kv': jax.random.normal(k2, (B, S, L), dtype=jnp.float32), 'Wq': jax.random.normal(k3, (H, H), dtype=jnp.float32) * scale, 'Wkv_expand': jax.random.normal(k4, (2 * H, L), dtype=jnp.float32) * scale, 'Wout': jax.random.normal(k5, (H, H), dtype=jnp.float32) * scale}
    _L0_xattn_all = _L0_xattn_setup()
    _L0_xattn_in = {k: v for k, v in _L0_xattn_all.items() if k in ('Wq', 'Wkv_expand', 'Wout')}
    del _L0_xattn_all

    def _L0_ffn_setup():
        import jax, jax.numpy as jnp
        import numpy as np
        TOP_K = 2
        key = jax.random.key(seed)
        ks = jax.random.split(key, 5)
        B, T, D, E, H = (4, 512, 512, 8, 352)
        s = 1.0 / np.sqrt(D)
        sh = 1.0 / np.sqrt(H)
        return {'x': jax.random.normal(ks[0], (B, T, D), dtype=jnp.float32), 'Wg': jax.random.normal(ks[1], (E, D), dtype=jnp.float32) * s, 'W1': jax.random.normal(ks[2], (E, H, D), dtype=jnp.float32) * s, 'W2': jax.random.normal(ks[3], (E, H, D), dtype=jnp.float32) * s, 'W3': jax.random.normal(ks[4], (E, D, H), dtype=jnp.float32) * sh}
    _L0_ffn_all = _L0_ffn_setup()
    _L0_ffn_in = {k: v for k, v in _L0_ffn_all.items() if k in ('Wg', 'W1', 'W2', 'W3')}
    del _L0_ffn_all

    def _L1_xattn_setup():
        import jax, jax.numpy as jnp
        import numpy as np
        B, S, L = (2, 256, 256)
        DIM_Q, H, K, D_C, D_CQ, R = (512, 16, 128, 128, 384, 64)

        def _rope_tables(seq_len, dim, dtype):
            inv_freq = 1.0 / 10000.0 ** (jnp.arange(0, dim, 2, dtype=dtype) / dim)
            t = jnp.arange(seq_len, dtype=dtype)
            freqs = t[:, None] * inv_freq[None, :]
            sin = jnp.repeat(jnp.sin(freqs), 2, axis=-1)
            cos = jnp.repeat(jnp.cos(freqs), 2, axis=-1)
            return (sin, cos)

        def _rotate_half(x):
            h = x.shape[-1] // 2
            return jnp.concatenate([-x[..., h:], x[..., :h]], axis=-1)
        key = jax.random.key(seed)
        ks = jax.random.split(key, 8)
        s_in = 1.0 / np.sqrt(DIM_Q)
        s_k = 1.0 / np.sqrt(K)
        s_cq = 1.0 / np.sqrt(D_CQ)
        s_c = 1.0 / np.sqrt(D_C)
        return {'hidden_q': jax.random.normal(ks[0], (B, S, DIM_Q), jnp.float32), 'kv_c': jax.random.normal(ks[1], (B, L, D_C), jnp.float32), 'Wq': jax.random.normal(ks[2], (H * K, DIM_Q), jnp.float32) * s_in, 'w_kc_q': jax.random.normal(ks[3], (H, K, D_CQ), jnp.float32) * s_k, 'w_kc_kv': jax.random.normal(ks[4], (H, K, D_C), jnp.float32) * s_k, 'W_qr': jax.random.normal(ks[5], (H, D_CQ, R), jnp.float32) * s_cq / np.sqrt(R), 'W_kr': jax.random.normal(ks[6], (H, D_C, R), jnp.float32) * s_c, 'Wo': jax.random.normal(ks[7], (DIM_Q, H * K), jnp.float32) * s_k}
    _L1_xattn_all = _L1_xattn_setup()
    _L1_xattn_in = {k: v for k, v in _L1_xattn_all.items() if k in ('Wq', 'w_kc_q', 'w_kc_kv', 'W_qr', 'W_kr', 'Wo')}
    del _L1_xattn_all

    def _L1_ffn_setup():
        import jax, jax.numpy as jnp
        import numpy as np
        QMAX = 127.0
        EPS = 1e-08

        def _quant_dequant(v, axis):
            scale = jnp.max(jnp.abs(v), axis=axis, keepdims=True) / QMAX
            scale = jnp.maximum(scale, EPS)
            q = jnp.clip(jnp.round(v / scale), -QMAX, QMAX)
            return q * scale

        def _ste(v, axis):
            return v + jax.lax.stop_gradient(_quant_dequant(v, axis) - v)
        key = jax.random.key(seed)
        k1, k2, k3 = jax.random.split(key, 3)
        H, I = (512, 1408)
        x = jax.random.normal(k1, (4, 512, H), dtype=jnp.float32)
        w_gate_up = jax.random.normal(k2, (2 * I, H), dtype=jnp.float32) * H ** (-0.5)
        w_down = jax.random.normal(k3, (H, I), dtype=jnp.float32) * I ** (-0.5)
        return {'x': x, 'w_gate_up': w_gate_up, 'w_down': w_down}
    _L1_ffn_all = _L1_ffn_setup()
    _L1_ffn_in = {k: v for k, v in _L1_ffn_all.items() if k in ('w_gate_up', 'w_down')}
    del _L1_ffn_all
    return {'x': x, 'ctx_512': ctx_512, 'L0_xattn_Wq': _L0_xattn_in['Wq'], 'L0_xattn_Wkv_expand': _L0_xattn_in['Wkv_expand'], 'L0_xattn_Wout': _L0_xattn_in['Wout'], 'L0_ffn_Wg': _L0_ffn_in['Wg'], 'L0_ffn_W1': _L0_ffn_in['W1'], 'L0_ffn_W2': _L0_ffn_in['W2'], 'L0_ffn_W3': _L0_ffn_in['W3'], 'L1_xattn_Wq': _L1_xattn_in['Wq'], 'L1_xattn_w_kc_q': _L1_xattn_in['w_kc_q'], 'L1_xattn_w_kc_kv': _L1_xattn_in['w_kc_kv'], 'L1_xattn_W_qr': _L1_xattn_in['W_qr'], 'L1_xattn_W_kr': _L1_xattn_in['W_kr'], 'L1_xattn_Wo': _L1_xattn_in['Wo'], 'L1_ffn_w_gate_up': _L1_ffn_in['w_gate_up'], 'L1_ffn_w_down': _L1_ffn_in['w_down']}

def reference(x, ctx_512, L0_xattn_Wq, L0_xattn_Wkv_expand, L0_xattn_Wout, L0_ffn_Wg, L0_ffn_W1, L0_ffn_W2, L0_ffn_W3, L1_xattn_Wq, L1_xattn_w_kc_q, L1_xattn_w_kc_kv, L1_xattn_W_qr, L1_xattn_W_kr, L1_xattn_Wo, L1_ffn_w_gate_up, L1_ffn_w_down):
    import jax
    import jax.numpy as jnp

    def _L0_xattn_ref(q, latent_kv, Wq, Wkv_expand, Wout):
        import jax, jax.numpy as jnp
        import numpy as np
        B, S, H, NH, L = (2, 512, 512, 16, 128)
        HD = H // NH
        b, sq, _ = q.shape
        sk = latent_kv.shape[1]
        qp = q @ Wq.T
        kv = latent_kv @ Wkv_expand.T
        k, v = jnp.split(kv, 2, axis=-1)
        qh = qp.reshape(b, sq, NH, HD).transpose(0, 2, 1, 3)
        kh = k.reshape(b, sk, NH, HD).transpose(0, 2, 1, 3)
        vh = v.reshape(b, sk, NH, HD).transpose(0, 2, 1, 3)
        inv_sqrt_d = 1.0 / jnp.sqrt(jnp.float32(HD))
        scores = jnp.einsum('bhqd,bhkd->bhqk', qh, kh) * inv_sqrt_d
        causal = jnp.tril(jnp.ones((sq, sk), dtype=bool))
        scores = jnp.where(causal, scores, jnp.finfo(scores.dtype).min)
        attn = jax.nn.softmax(scores, axis=-1)
        out = jnp.einsum('bhqk,bhkd->bhqd', attn, vh)
        out = out.transpose(0, 2, 1, 3).reshape(b, sq, H)
        return out @ Wout.T

    def _L0_ffn_ref(x, Wg, W1, W2, W3):
        import jax, jax.numpy as jnp
        import numpy as np
        TOP_K = 2
        E = Wg.shape[0]
        scores = jnp.einsum('btd,ed->bte', x, Wg)
        topk_s, topk_i = jax.lax.top_k(scores, TOP_K)
        probs = jax.nn.softmax(topk_s, axis=-1)
        onehot = (topk_i[..., None] == jnp.arange(E)).astype(x.dtype)
        w = jnp.einsum('btk,btke->bte', probs, onehot)
        y = jnp.zeros_like(x)
        for e in range(E):
            h = jax.nn.silu(jnp.einsum('btd,hd->bth', x, W1[e])) * jnp.einsum('btd,hd->bth', x, W2[e])
            y = y + w[..., e:e + 1] * jnp.einsum('bth,dh->btd', h, W3[e])
        return y

    def _L1_xattn_ref(hidden_q, kv_c, Wq, w_kc_q, w_kc_kv, W_qr, W_kr, Wo):
        import jax, jax.numpy as jnp
        import numpy as np
        B, S, L = (2, 256, 256)
        DIM_Q, H, K, D_C, D_CQ, R = (512, 16, 128, 128, 384, 64)

        def _rope_tables(seq_len, dim, dtype):
            inv_freq = 1.0 / 10000.0 ** (jnp.arange(0, dim, 2, dtype=dtype) / dim)
            t = jnp.arange(seq_len, dtype=dtype)
            freqs = t[:, None] * inv_freq[None, :]
            sin = jnp.repeat(jnp.sin(freqs), 2, axis=-1)
            cos = jnp.repeat(jnp.cos(freqs), 2, axis=-1)
            return (sin, cos)

        def _rotate_half(x):
            h = x.shape[-1] // 2
            return jnp.concatenate([-x[..., h:], x[..., :h]], axis=-1)
        b, s, _ = hidden_q.shape
        l = kv_c.shape[1]
        q_hk = (hidden_q @ Wq.T).reshape(b, s, H, K)
        q_big = jnp.einsum('bshk,hkq->bshq', q_hk, w_kc_q)
        sin, cos = _rope_tables(l, D_C, kv_c.dtype)
        kv_rope = kv_c * cos[None] + _rotate_half(kv_c) * sin[None]
        q_r = jnp.einsum('bshq,hqr->bhsr', q_big, W_qr)
        k_r = jnp.einsum('bld,hdr->bhlr', kv_rope, W_kr)
        scores = jnp.einsum('bhsr,bhlr->bhsl', q_r, k_r)
        attn = jax.nn.softmax(scores, axis=-1)
        ctx_c = jnp.einsum('bhsl,bld->bhsd', attn, kv_rope)
        ctx_lat = jnp.einsum('bhsd,hkd->bshk', ctx_c, w_kc_kv)
        out = ctx_lat.reshape(b, s, H * K) @ Wo.T
        return out

    def _L1_ffn_ref(x, w_gate_up, w_down):
        import jax, jax.numpy as jnp
        import numpy as np
        QMAX = 127.0
        EPS = 1e-08

        def _quant_dequant(v, axis):
            scale = jnp.max(jnp.abs(v), axis=axis, keepdims=True) / QMAX
            scale = jnp.maximum(scale, EPS)
            q = jnp.clip(jnp.round(v / scale), -QMAX, QMAX)
            return q * scale

        def _ste(v, axis):
            return v + jax.lax.stop_gradient(_quant_dequant(v, axis) - v)
        I = w_down.shape[1]
        xq = _ste(x, axis=-1)
        w1q = _ste(w_gate_up, axis=-1)
        gate_up = jnp.einsum('bsh,oh->bso', xq, w1q)
        gate, up = (gate_up[..., :I], gate_up[..., I:])
        h = jax.nn.silu(gate) * up
        hq = _ste(h, axis=-1)
        w2q = _ste(w_down, axis=-1)
        return jnp.einsum('bsi,oi->bso', hq, w2q)
    x = x + _L0_xattn_ref(_layernorm(x, axis=-1), ctx_512, L0_xattn_Wq, L0_xattn_Wkv_expand, L0_xattn_Wout)
    x = x + _L0_ffn_ref(_layernorm(x, axis=-1), L0_ffn_Wg, L0_ffn_W1, L0_ffn_W2, L0_ffn_W3)
    x = x + _L1_xattn_ref(_layernorm(x, axis=-1), ctx_512, L1_xattn_Wq, L1_xattn_w_kc_q, L1_xattn_w_kc_kv, L1_xattn_W_qr, L1_xattn_W_kr, L1_xattn_Wo)
    x = x + _L1_ffn_ref(_layernorm(x, axis=-1), L1_ffn_w_gate_up, L1_ffn_w_down)
    return x

_drawn_inputs = setup_inputs


def setup_inputs(seed=0):
    import zlib

    import numpy as np

    out = dict(_drawn_inputs(seed))
    spreads = {}
    factors = {'L0_xattn_Wq': 4.658}
    for name, (base, spread) in spreads.items():
        noise = np.random.default_rng([zlib.crc32(name.encode()), seed]).standard_normal(out[name].shape)
        drawn = base * np.exp(spread * noise) if base else spread * noise
        out[name] = jnp.asarray(drawn.astype(out[name].dtype))
    for name, factor in factors.items():
        out[name] = (out[name] * factor).astype(out[name].dtype)
    return out
```

```python
import itertools
from contextlib import ExitStack

import numpy as np

import concourse.bass as bass
from concourse import mybir

F32 = mybir.dt.float32
F32R = mybir.dt.float32r
BF16 = mybir.dt.bfloat16
U32 = mybir.dt.uint32
ALU = mybir.AluOpType
ACT = mybir.ActivationFunctionType
AX = mybir.AxisListType

B, T, D = 8, 100, 512
KC = D // 128
LN_EPS = 1e-5
NH0, HD0, LAT = 16, 32, 128
HG = 128 // HD0
MT0 = NH0 // HG
NE, FH = 8, 352
FC = [128, 128, FH - 256]
HALF = B // 2 * T
W12, W3 = 2 * KC * FH, len(FC) * D
FI = 1408
IC = FI // 128
UT, DT = 2 * FI // 128, D // 128
GC = 4
GW_ = FI // GC
QMAX, QEPS = 127.0, 1e-8
MAGIC = 1.5 * 2 ** 23
NK, DK, LK, R1, CQ = 361, 128, 3, 64, 384
NP1 = NH0 // 2
ROWS = NH0 * T
RT = -(-ROWS // 128)
NG = -(-RT // 4)
LAG = 5
PVLAG = 2
ROPE_AT = [0, 1, 2, 4]
KVAT = LAG + 5
KBANK = 4 + (KVAT - LAG) % 3
NKE = NK + 1
FQ = LK * DK + LK * R1 + D
FP = DK + D


def layer_norm_steps(X, stats, mv, veps, std, rstd, s, ph):

    def vector(dve):
        for b in range(B):
            dve.bn_stats(stats[:, b, :], X[:, b, :]).then_inc(s["stats"], 1)
        dve.wait_ge(s["stats"], B * (ph + 1))
        for b in range(B):
            dve.bn_aggr(mv[:, b, :], stats[:, b, :]).then_inc(s["moments"], 1)
        dve.wait_ge(s["moments"], B * (ph + 1))
        dve.tensor_scalar(veps[:, :], mv[:, :, 1], LN_EPS, None, ALU.add).then_inc(s["var"], 1)
        dve.wait_ge(s["std"], ph + 1)
        dve.reciprocal(rstd[:, :], std[:, :]).then_inc(s["rstd"], 1)
        dve.wait_ge(s["rstd"], ph + 1)

    def scalar(act):
        act.wait_ge(s["var"], ph + 1)
        act.activation(std[:, :], veps[:, :], ACT.Sqrt).then_inc(s["std"], 1)

    return vector, scalar


def build_kernel(nc, x, ctx_t, wq0_t, wkv0_t, wout0_t, ident_d, mask_d, wg_t, w12_d, w3_d, iota_d,
                 ctxn_d, cos_d, sin_d, foldq_d, krt_d, foldp_d,
                 wup_d, wdown_d, out):
    with ExitStack() as top:
        def sem(name):
            return top.enter_context(nc.semaphore(name))

        def sems(phase, names):
            return {n: sem(f"{phase}_{n}") for n in names.split()}

        def sb_in(stack):
            return lambda name, shape, dt=F32: stack.enter_context(nc.sbuf_tensor(name, shape, dt))

        def ln_transposes(pe, ph, b):
            pe.wait_ge(LN["xn"], B * ph + b + 1)
            wait(pe, LN["lo"], B * ph + b - 1)
            for k in range(KC):
                last = pe.transpose(TP[b % 2][:, k, :], xn[:, b % 2, k * 128:(k + 1) * 128], ident[0:T, 0:T])
            last.then_inc(LN["xnt"], 1)

        def ln_high(act, ph, b, xh):
            act.wait_ge(LN["xnt"], B * ph + b + 1)
            act.copy(xh[:, :, b * T:(b + 1) * T], TP[b % 2]).then_inc(LN["hi"], 1)

        def ln_low(dve, ph, b, xh, xl):
            dve.wait_ge(LN["hi"], B * ph + b + 1)
            t = slice(b * T, (b + 1) * T)
            dve.tensor_tensor(xl[:, :, t], TP[b % 2], xh[:, :, t].bitcast(F32), ALU.subtract).then_inc(LN["lo"], 1)

        def normalise(dve, ph, b):
            wait(dve, LN["xnt"], B * ph + b - 1)
            dve.tensor_scalar(xn[:, b % 2, :], X[:, b, :], mv[:, b, 0:1], rstd[:, b:b + 1],
                              ALU.subtract, ALU.mult).then_inc(LN["xn"], 1)

        numbers = itertools.count()

        def wait(e, s, v):
            if isinstance(v, int):
                if v > 0:
                    e.wait_ge(s, v)
            elif v.min_val >= 0:
                e.wait_ge(s, v)
            else:
                count = e.alloc_register(f"count{next(numbers)}")
                e.reg_alu(count, v, 0, ALU.max)
                e.wait_ge(s, count)
                e.free_register(count)

        def mm3(pe, o, lh, ll, rh, rl, start, stop):
            pe.matmul(o, lh, rh, start=start, stop=False)
            pe.matmul(o, lh, rl, start=False, stop=False)
            return pe.matmul(o, ll, rh, start=False, stop=stop)

        sb = sb_in(top)
        X = sb("X", [T, B, D])
        ident = sb("ident", [128, 128])
        identb = sb("identb", [128, 128], BF16)
        stats = sb("stats", [T, B, 6])
        mv = sb("mv", [T, B, 2])
        veps = sb("veps", [T, B])
        std = sb("std", [T, B])
        rstd = sb("rstd", [T, B])
        xn = sb("xn", [T, 2, D])
        iota = sb("iota", [T, NE])
        wg = [sb("wg_raw", [128, KC, NE])] + [sb(f"wg_{n}", [128, KC, NE], F32R) for n in ("hi", "lo")]
        wraw = sb("wraw", [128, W12 + W3])
        PS = top.enter_context(nc.psum_tensor("PS", [128, 8, 512], F32))

        pa = ExitStack()
        sa = sb_in(pa)
        NCX = B * T
        XH = sa("xnT_hi", [128, KC, NCX], F32R)
        XL = sa("xnT_lo", [128, KC, NCX], F32R)
        RAW_CTX, RAW_WKV, RAW_WQ, RAW_WO = 0, NCX, NCX + 2 * D, NCX + 2 * D + KC * D
        RAW_N = RAW_WO + KC * D
        raw0 = sa("raw0", [128, RAW_N])
        hi0 = sa("hi0", [128, RAW_N], F32R)
        lo0 = sa("lo0", [128, RAW_N], F32R)
        mask_f = sa("mask_f", [T, T])
        maskb = sa("maskb", [T, T], BF16)
        V = sa("V", [T, B, NH0, HD0 + 1])
        QT = sa("QT", [128, MT0, 2, T])
        KT = sa("KT", [128, MT0, 2, T])
        P0 = [sa(f"P0_{i}", [T, HG, MT0, T]) for i in range(2)]
        mx0 = sa("mx0", [T, 2, HG, MT0])
        PT = sa("PT0", [T, HG, MT0, T])
        rs0 = sa("rs0", [T, HG, MT0])
        O0 = sa("O0", [T, D])
        OH = sa("OH", [128, KC, T], F32R)
        OL = sa("OL", [128, KC, T], F32R)
        pa.close()

        pb = ExitStack()
        sbb = sb_in(pb)
        XHB = sbb("xnTb_hi", [128, KC, NCX], F32R)
        XLB = sbb("xnTb_lo", [128, KC, NCX], F32R)
        logits = sbb("logits", [T, B, NE])
        top8 = sbb("top8", [T, B, 8])
        top8i = sbb("top8i", [T, B, 8], U32)
        top2i = sbb("top2i", [T, B, 2])
        gd = sbb("gd", [T, 4, B])
        geq = sbb("geq", [T, 4, B, NE])
        GW = sbb("GW", [T, NE, B])
        wh = [sbb(f"we_hi{i}", [128, W12 + W3], F32R) for i in range(2)]
        wl = [sbb(f"we_lo{i}", [128, W12 + W3], F32R) for i in range(2)]
        silu = sbb("silu", [128, 2, HALF])
        h32 = sbb("h32", [128, 2, HALF])
        HH = sbb("hT_hi", [128, len(FC), NCX], F32R)
        HL = sbb("hT_lo", [128, len(FC), NCX], F32R)
        pb.close()

        pc = ExitStack()
        sc_ = sb_in(pc)
        XHC = sc_("xnTc_hi", [128, KC, NCX], F32R)
        XLC = sc_("xnTc_lo", [128, KC, NCX], F32R)
        NFH = sc_("nf_hi", [128, KC, NP1 * 128], F32R)
        NFL = sc_("nf_lo", [128, KC, NP1 * 128], F32R)
        WKH = sc_("wkr_hi", [128, NP1, DK], F32R)
        WKL = sc_("wkr_lo", [128, NP1, DK], F32R)
        QRH = sc_("qr_hi", [128, NP1, 2 * T], F32R)
        QRL = sc_("qr_lo", [128, NP1, 2 * T], F32R)
        QH = sc_("q_hi", [128, 2, ROWS], F32R)
        QL = sc_("q_lo", [128, 2, ROWS], F32R)
        cosr = sc_("cosr", [128, LK, DK])
        sinr = sc_("sinr", [128, LK, DK])
        kvraw = [sc_(f"kvraw{i}", [128, LK, DK]) for i in range(2)]
        kvt = [sc_(f"kvt{i}", [128, LK, DK]) for i in range(2)]
        kvr = sc_("kvr", [128, LK, DK])
        KNH = [sc_(f"kn_hi{i}", [128, LK, DK], F32R) for i in range(2)]
        KNL = [sc_(f"kn_lo{i}", [128, LK, DK], F32R) for i in range(2)]
        KTH = [sc_(f"kt_hi{i}", [128, NKE], F32R) for i in range(2)]
        KTL = [sc_(f"kt_lo{i}", [128, NKE], F32R) for i in range(2)]
        nmx = sc_("nmx", [128, 2, RT])
        rsum = sc_("rsum", [128, 2, RT])
        rinv = sc_("rinv", [128, 2, RT])
        ctxo = [sc_(f"ctxo{i}", [128, 512]) for i in range(2)]
        m_sb = [sc_(f"m_sb{i}", [128, 2, R1]) for i in range(2)]
        early = ExitStack()
        kr_raw = early.enter_context(nc.sbuf_tensor("kr_raw", [128, NP1, DK], F32))
        early.close()
        PTH = [sc_(f"pt_hi{i}", [128, LK, 512], F32R) for i in range(2)]
        PTL = [sc_(f"pt_lo{i}", [128, LK, 512], F32R) for i in range(2)]
        PTH.append(sc_("pt_hi_end", [128, LK, ROWS % 512], F32R))
        PTL.append(sc_("pt_lo_end", [128, LK, ROWS % 512], F32R))
        pc.close()
        P1 = [wraw[:, i * 384:(i + 1) * 384] for i in range(8)]
        FQR = [wraw[:, i * 2 * FQ:(i + 1) * 2 * FQ].rearrange("p (h n) -> p h n", h=2) for i in range(2)]

        pd = ExitStack()
        sd = sb_in(pd)
        PFH = sd("pf_hi", [128, NH0, D], F32R)
        PFL = sd("pf_lo", [128, NH0, D], F32R)
        CXR = [sd(f"cx_raw{i}", [128, ROWS]) for i in range(2)]
        CXH = [sd(f"cx_hi{i}", [128, ROWS], F32R) for i in range(2)]
        CXL = [sd(f"cx_lo{i}", [128, ROWS], F32R) for i in range(2)]
        W1Q = sd("w1q", [128, KC, 2 * FI], BF16)
        W2Q = sd("w2q", [128, IC, D], BF16)
        S1B = sd("s1_rows", [T, 2 * FI])
        S2B = sd("s2_rows", [T, D])
        ones = sd("ones", [128, T])
        WQT = [sd(f"wq_tile{i}", [128, FI], BF16) for i in range(3)]
        wsc = [sd(f"wscale{i}", [128, 3]) for i in range(3)]
        diag = [sd(f"wdiag{i}", [128, 128]) for i in range(3)]
        mgc = sd("mgc", [128, 1])
        pd.close()
        WRT = [wraw[:, i * FI:(i + 1) * FI] for i in range(3)]
        pf_ = ExitStack()
        sf = sb_in(pf_)
        XM = [sf(f"xm{i}", [T, D]) for i in range(2)]
        XQ = [sf(f"xq{i}", [T, D], BF16) for i in range(2)]
        XQT = [sf(f"xqt{i}", [128, KC, T], BF16) for i in range(2)]
        sx = sf("sx", [T, 2, 3])
        sh = sf("sh", [T, 2, 4])
        GS = [sf(f"gs{i}", [T, GW_]) for i in range(2)]
        SL = [sf(f"sl{i}", [T, GW_]) for i in range(2)]
        US = [sf(f"us{i}", [T, GW_]) for i in range(2)]
        H1 = [sf(f"h1_{i}", [T, FI]) for i in range(2)]
        HQ = [sf(f"hq{i}", [T, FI], BF16) for i in range(2)]
        HQT = [sf(f"hqt{i}", [128, IC, T], BF16) for i in range(2)]
        Y2 = [sf(f"y2_{i}", [T, D]) for i in range(2)]
        pf_.close()
        FPR = [wraw[:, i * 2 * FP:(i + 1) * 2 * FP].rearrange("p (h n) -> p h n", h=2) for i in range(2)]
        ctx_scratch = nc.dram_tensor("ctx_scratch", [B, 128, ROWS], F32, kind="Internal").ap()

        C = sems("c", "fq0 fq1 m msb nf nfh nfl kr krh krl cs kvz kv0 kv1 rot kvr "
                      "knh knl ktp kth ktl pr prh prl s max exp inv nrm pt pth ptl pv ctxo st0 st1")
        O = sems("o", "fp0 fp1 pf pfh pfl cx0 cx1 cxh cxl out res")

        LN = sems("ln", "stats moments var std rstd xn xnt hi lo")
        W = sems("w", "ld0 ld1 ld2 max sc inv mag sub tr ev dg bc sb ones mgc")
        F = sems("f", "xn xscale inv mag sub xt xev gps ups gs silu us h hscale hinv hmag "
                      "hsub ht hev dn y res")

        A = sems("a", "x consts wctx wwkv wwq wwo "
                      "cast whi wlo vones vps vsb qk qsb ksb sc mx sub exp pt ptsb pv rs onorm ot oh ol op res")

        E = sems("e", "consts wghi wglo gate logits gating diff ex "
                      "d12 d3 hi12 lo12 hi3 lo3 gps ups silu hmul hhi hlo yps yacc zero")

        def part(t, at, *dims):
            n = int(np.prod(dims))
            v = t[:, at:at + n]
            if len(dims) == 2:
                return v.rearrange("p (a b) -> p a b", a=dims[0])
            return v

        wqh, wql = (part(t, RAW_WQ, KC, D) for t in (hi0, lo0))
        woh, wol = (part(t, RAW_WO, KC, D) for t in (hi0, lo0))
        wkvh, wkvl = (part(t, RAW_WKV, 2 * D) for t in (hi0, lo0))
        cxh, cxl = (part(t, RAW_CTX, B, T) for t in (hi0, lo0))
        SPLITS = [(RAW_CTX, RAW_WKV, "wctx"), (RAW_WKV, RAW_WQ, "wwkv"), (RAW_WQ, RAW_WO, "wwq"), (RAW_WO, RAW_N, "wwo")]
        S0 = [PS[0:T, i, 0:MT0 * T].rearrange("p (m k) -> p m k", m=MT0) for i in range(HG)]
        TP = [PS[:, 4, 0:KC * T].rearrange("p (m k) -> p m k", m=KC), PS[:, 5, 0:KC * T].rearrange("p (m k) -> p m k", m=KC)]
        OV = [PS[0:T, 6 + i, 0:2 * MT0 * (HD0 + 1)].rearrange("p (i m d) -> p i m d", i=2, m=MT0) for i in range(2)]
        INV0 = 1.0 / float(np.sqrt(np.float32(HD0)))
        ln_vec, ln_act = layer_norm_steps(X, stats, mv, veps, std, rstd, LN, 0)
        lnf_vec, lnf_act = layer_norm_steps(X, stats, mv, veps, std, rstd, LN, 3)
        lnc_vec, lnc_act = layer_norm_steps(X, stats, mv, veps, std, rstd, LN, 2)
        lne_vec, lne_act = layer_norm_steps(X, stats, mv, veps, std, rstd, LN, 1)

        def w12_of(t, which, k, c):
            at = (which * KC + k) * FH + c * 128
            return t[:, at:at + FC[c]]

        def w3_of(t, c):
            return t[0:FC[c], W12 + c * D:W12 + (c + 1) * D]

        def pair_steps(last, vector):
            ticks = [("S", b, t) for b in range(2) for t in range(RT)]
            ticks += [("PR", 2, k) for k in range(12)] if not last else []
            delay = {"PT": 1, "KV": 1, "PV": 1} if vector else {}
            due = []
            for b in range(2):
                for t in range(RT):
                    at = RT * b + t
                    at = at + LAG if at + LAG < 2 * RT else 2 * RT + 2 * (at + LAG - 2 * RT)
                    due.append((at, 1, ("PT", b, t)))
                    if t % 4 == 3:
                        due += [(at + PVLAG + c, 0, ("PV", b, t // 4 * LK + c)) for c in range(LK)]
                    elif t == RT - 1:
                        due += [(at + PVLAG + 2, 0, ("PV", b, t // 4 * LK + c)) for c in range(LK)]
                if b == 0 or not last:
                    due.append((RT * b + KVAT - 1, 2, ("KV", b + 1, 0)))
            placed = sorted((at + (delay.get(step[0], 0) if at + delay.get(step[0], 0) < 2 * RT else 0), at, order, step)
                            for at, order, step in due)
            out = []
            for i, tick in enumerate(ticks):
                out.append(tick)
                out += [step for at, _, _, step in placed if at == i]
            return out + [step for at, _, _, step in placed if at >= len(ticks)]

        def attention_steps(kind, vector=False):
            steps = pair_steps(kind == "last", vector)
            cut = steps.index(("S", 1, 0))
            steps = steps[:cut] if kind == "even" else [(w, b - 1, t) for w, b, t in steps[cut:]]
            return [(w, b, t) for w, b, t in steps]

        HTG = [(0, 6), (6, IC)]

        def earlier(t, ring):
            return t - ring if t >= ring else max(u for u in range(RT) if u % ring == t) - RT

        def tile_rows(t):
            return min(128, ROWS - 128 * t)

        def wtiles(n, odd):
            if isinstance(n, int) and n == B:
                return [("up", UT - 2), ("up", UT - 1)]
            p = (n[0] if isinstance(n, tuple) else n // 2)
            return [("up", 5 * p + 3), ("up", 5 * p + 4), ("down", p)] if odd else [("up", 5 * p + i) for i in range(3)]

        def cols_at(i, width):
            return slice(i * width, (i + 1) * width) if isinstance(i, int) else bass.ds(i * width, width)

        def wbank(i, chunks):
            b = PS[:, i, :] if i < 2 else PS[:, 2:4, :].rearrange("p a n -> p (a n)")
            return b.bitcast(BF16)[:, 0:chunks * 128].rearrange("p (c n) -> p c n", c=chunks)

        OUTS = [sem("out_stored0"), sem("out_stored1")]
        block = top.enter_context(nc.Block())

        @block.sync
        def _(sp):
            xr = x.rearrange("b t d -> t b d")
            sp.dma_start(X[:, 0:B // 2, :], xr[:, 0:B // 2, :]).then_inc(A["x"], 16)
            sp.dma_start(X[:, B // 2:B, :], xr[:, B // 2:B, :]).then_inc(A["x"], 16)
            sp.dma_start(ident[:, :], ident_d).then_inc(A["consts"], 16)
            sp.dma_start(mask_f[:, :], mask_d).then_inc(A["consts"], 16)
            sp.dma_start(part(raw0, RAW_CTX, B, T), ctx_t[:, :, 0:T]).then_inc(A["wctx"], 16)
            sp.dma_start(part(raw0, RAW_WKV, 2 * D), wkv0_t).then_inc(A["wwkv"], 16)
            sp.dma_start(part(raw0, RAW_WQ, KC * D), wq0_t).then_inc(A["wwq"], 16)
            sp.dma_start(part(raw0, RAW_WO, KC * D), wout0_t).then_inc(A["wwo"], 16)
            sp.dma_start(iota[:, :], iota_d).then_inc(E["consts"], 16)
            sp.dma_start(wg[0][:, :, :], wg_t).then_inc(E["consts"], 16)

            def load_expert(e):
                w12s = w12_d[e] if isinstance(e, int) else w12_d[bass.ds(e, 1)].rearrange("o p n -> (o p) n")
                w3s = w3_d[e] if isinstance(e, int) else w3_d[bass.ds(e, 1)].rearrange("o h n -> (o h) n")
                wait(sp, E["lo12"], e)
                sp.dma_start(wraw[:, 0:W12], w12s).then_inc(E["d12"], 16)
                wait(sp, E["lo3"], e)
                whole = len(FC) - 1
                if isinstance(e, int) and e == 0:
                    sp.wait_ge(E["zero"], 1)
                sp.dma_start(wraw[:, W12:W12 + whole * D].rearrange("p (c n) -> p c n", c=whole),
                             w3s[0:whole * 128].rearrange("(c p) n -> p c n", p=128)).then_inc(E["d3"], 16)
                sp.dma_start(wraw[0:FC[-1], W12 + whole * D:W12 + W3], w3s[whole * 128:FH]).then_inc(E["d3"], 16)

            load_expert(0)
            with sp.Fori(1, NE) as e:
                load_expert(e)
            sp.wait_ge(E["yacc"], B * NE)
            sp.dma_start(kr_raw[:, :, :], krt_d).then_inc(C["kr"], 16)
            sp.dma_start(cosr[:, :, :], cos_d).then_inc(C["cs"], 16)
            sp.dma_start(sinr[:, :, :], sin_d).then_inc(C["cs"], 16)

            def load_foldq(i, j):
                wait(sp, C["nf"], i - 1)
                sp.dma_start(FQR[j], (foldq_d[i] if isinstance(i, int) else
                                      foldq_d[bass.ds(i, 1)].rearrange("o p h n -> (o p) h n"))).then_inc(C[f"fq{j}"], 16)

            load_foldq(0, 0)
            load_foldq(1, 1)

            def load_kv(n, j):
                if isinstance(n, int) and n < 2:
                    sp.wait_ge(C["kvz"], 2)
                wait(sp, C["rot"], 3 * (n - 1))
                kvn = ctxn_d[n] if isinstance(n, int) else ctxn_d[bass.ds(n, 1)].rearrange("o l d -> (o l) d")
                whole = LK - 1
                sp.dma_start(kvraw[j][:, 0:whole, :], kvn[0:whole * 128].rearrange("(c p) d -> p c d", p=128)) \
                    .then_inc(C[f"kv{j}"], 16)
                sp.dma_start(kvraw[j][0:NK - whole * 128, whole, :], kvn[whole * 128:NK]).then_inc(C[f"kv{j}"], 16)

            load_kv(0, 0)
            load_kv(1, 1)
            with sp.Fori(1, NP1 // 2) as i:
                load_foldq(2 * i, 0)
                load_foldq(2 * i + 1, 1)

            def store_ctx(n, g):
                cols = min(512, ROWS - g * 512)
                wait(sp, C["ctxo"], NG * n + g + 1)
                dst = ctx_scratch[n] if isinstance(n, int) else ctx_scratch[bass.ds(n, 1)].rearrange("o p r -> (o p) r")
                sp.dma_start(dst[:, g * 512:g * 512 + cols], ctxo[g % 2][:, 0:cols]).then_inc(C[f"st{g % 2}"], 16)

            def store_batch(n, j, more=True):
                if more:
                    load_kv(n + 2, j)
                for g in range(NG):
                    store_ctx(n, g)

            with sp.Fori(0, B // 2 - 1) as p:
                store_batch(2 * p, 0)
                store_batch(2 * p + 1, 1)
            store_batch(B - 2, 0, False)
            store_batch(B - 1, 1, False)

            def load_foldp(i, j):
                if isinstance(i, int) and i < 2:
                    wait(sp, C["pt"], RT * B)
                wait(sp, O["pf"], 2 * (i - 1))
                sp.dma_start(FPR[j], (foldp_d[i] if isinstance(i, int) else
                                      foldp_d[bass.ds(i, 1)].rearrange("o p h n -> (o p) h n"))).then_inc(O[f"fp{j}"], 16)

            def load_ctx(n, j):
                if isinstance(n, int) and n == 0:
                    sp.wait_ge(C["st0"], 16 * NG // 2 * B)
                    sp.wait_ge(C["st1"], 16 * NG // 2 * B)
                wait(sp, O["cxl"], n - 1)
                src = ctx_scratch[n] if isinstance(n, int) else ctx_scratch[bass.ds(n, 1)].rearrange("o p r -> (o p) r")
                sp.dma_start(CXR[j][:, :], src).then_inc(O[f"cx{j}"], 16)

            load_foldp(0, 0)
            load_foldp(1, 1)
            load_ctx(0, 0)
            load_ctx(1, 1)
            with sp.Fori(1, NP1 // 2) as i:
                load_foldp(2 * i, 0)
                load_foldp(2 * i + 1, 1)
            with sp.Fori(1, B // 2) as p:
                load_ctx(2 * p, 0)
                load_ctx(2 * p + 1, 1)
            def store_out(n, j):
                wait(sp, F["res"], n + 1)
                o = out[n] if isinstance(n, int) else out[bass.ds(n, 1)].rearrange("o t d -> (o t) d")
                xs = X[:, n, :] if isinstance(n, int) else X[:, bass.ds(n, 1), :].rearrange("p a d -> p (a d)")
                sp.dma_start(o, xs).then_inc(OUTS[j], 16)

            with sp.Fori(0, B // 2) as p:
                store_out(2 * p, 0)
                store_out(2 * p + 1, 1)
            sp.wait_ge(OUTS[0], 16 * B // 2)
            sp.wait_ge(OUTS[1], 16 * B // 2)

        @block.gpsimd
        def _(pool):
            pool.wait_ge(A["consts"], 32)
            pool.tensor_copy(identb[:, :], ident[:, :]).then_inc(A["cast"], 1)
            pool.tensor_copy(maskb[:, :], mask_f[:, :]).then_inc(A["cast"], 1)
            pool.memset(V[:, :, :, :], 1.0).then_inc(A["vones"], 1)
            pool.wait_ge(A["vones"], 1)
            pool.memset(wraw[FC[-1]:128, W12 + (len(FC) - 1) * D:W12 + W3], 0.0).then_inc(E["zero"], 1)
            pool.wait_ge(E["zero"], 1)

            def split_low(e, j):
                wait(pool, E["hi12"], e + 1)
                pool.tensor_tensor(wl[j][:, 0:W12], wraw[:, 0:W12], wh[j][:, 0:W12].bitcast(F32), ALU.subtract) \
                    .then_inc(E["lo12"], 1)
                wait(pool, E["hi3"], e + 1)
                pool.tensor_tensor(wl[j][:, W12:], wraw[:, W12:], wh[j][:, W12:].bitcast(F32), ALU.subtract) \
                    .then_inc(E["lo3"], 1)

            with pool.Fori(0, NE // 2) as i:
                split_low(2 * i, 0)
                split_low(2 * i + 1, 1)

            pool.wait_ge(E["yacc"], B * NE)
            tail = (NK - 256) // 32 * 32
            for j in range(2):
                pool.memset(kvraw[j][tail:128, LK - 1, :], 0.0).then_inc(C["kvz"], 1)
                pool.wait_ge(C["kvz"], j + 1)

            def rope(n, j, part):
                h = DK // 2
                if part == 0:
                    wait(pool, C[f"kv{j}"], 16 * n + 32 - 16 * j)
                    if isinstance(n, int) and n == 0:
                        pool.wait_ge(C["cs"], 32)
                    wait(pool, C["kvr"], n)
                    pool.tensor_tensor(kvt[0][:, :, :], kvraw[j][:, :, :], cosr[:, :, :], ALU.mult).then_inc(C["rot"], 1)
                elif part == 1:
                    pool.tensor_tensor(kvt[1][:, :, 0:h], kvraw[j][:, :, h:DK], sinr[:, :, 0:h], ALU.mult).then_inc(C["rot"], 1)
                elif part == 2:
                    pool.tensor_tensor(kvt[1][:, :, h:DK], kvraw[j][:, :, 0:h], sinr[:, :, h:DK], ALU.mult).then_inc(C["rot"], 1)
                else:
                    wait(pool, C["rot"], 3 * n + 3)
                    wait(pool, C["ktp"], n)
                    wait(pool, C["knl"], n)
                    pool.tensor_tensor(kvr[:, :, :], kvt[0][:, :, :], kvt[1][:, :, :], ALU.add).then_inc(C["kvr"], 1)

            def rope_low(n, j):
                wait(pool, C["knh"], n + 1)
                pool.tensor_tensor(KNL[j][:, :, :], kvr[:, :, :], KNH[j][:, :, :].bitcast(F32), ALU.subtract).then_inc(C["knl"], 1)

            def pool_steps(kind, n, j):
                for step in attention_steps(kind):
                    what, dn, t = step
                    m, jj = (n, j) if dn == 0 else (n + dn, 1 - j)
                    if what == "S":
                        rows = min(128, ROWS - 128 * t)
                        slot = t % 8
                        wait(pool, C["inv"], RT * m + t + 1)
                        pool.tensor_tensor(P1[slot][0:rows, 0:NK], P1[slot][0:rows, 0:NK],
                                           rinv[0:rows, jj, t:t + 1].broadcast_to((rows, NK)), ALU.mult).then_inc(C["nrm"], 1)
                        if kind != "last" and t in ROPE_AT:
                            rope(n + 1, 1 - j, ROPE_AT.index(t))
                    elif what == "KV":
                        rope_low(n + 1, 1 - j)

            wait(pool, C["nf"], NP1)
            for slot in range(8):
                pool.memset(P1[slot][:, NK:384], 0.0).then_inc(C["kvz"], 1)
            pool.wait_ge(C["kvz"], 10)
            for part in range(4):
                rope(0, 0, part)
            rope_low(0, 0)
            pool_steps("even", 0, 0)
            with pool.Fori(0, B // 2 - 1) as p:
                pool_steps("odd", 2 * p + 1, 1)
                pool_steps("even", 2 * p + 2, 0)
            pool_steps("last", B - 1, 1)

            def load_tile(n, i, kind, at):
                wait(pool, W["sub"], 3 * (n - 1) + i + 1)
                if kind == "up":
                    src, dst = wup_d, WRT[i][:, 0:D]
                else:
                    src, dst = wdown_d, WRT[i]
                pool.dma_start(dst, src[cols_at(at, 128), :]).then_inc(W[f"ld{i}"], 16)

            def diagonal(n, i):
                wait(pool, W["sc"], 3 * n + i + 1)
                wait(pool, W["bc"], 3 * (n - 1) + i + 1)
                pool.tensor_tensor(diag[i][:, :], ident[:, :], wsc[i][:, 1:2].broadcast_to((128, 128)), ALU.mult) \
                    .then_inc(W["dg"], 1)

            def pool_weights(n, odd, p=None, more=None):
                for i, _ in enumerate(wtiles(n if p is None else (p,), odd)):
                    diagonal(n, i)
                if more is not None:
                    for i, (kind, at) in enumerate(more):
                        load_tile(n + 1, i, kind, at)

            pool.wait_ge(O["pf"], NH0)
            pool.memset(ones[:, :], 1.0).then_inc(W["ones"], 1)
            pool.wait_ge(W["ones"], 1)
            pool.memset(mgc[:, :], MAGIC).then_inc(W["mgc"], 1)
            pool.wait_ge(W["mgc"], 1)
            for i, (kind, at) in enumerate(wtiles(0, False)):
                load_tile(0, i, kind, at)
            with pool.Fori(0, B // 2 - 1) as p:
                pool_weights(2 * p, False, p, wtiles((p,), True))
                pool_weights(2 * p + 1, True, p, wtiles((p + 1,), False))
            pool_weights(B - 2, False, None, wtiles(B - 1, True))
            pool_weights(B - 1, True, None, wtiles(B, False))
            pool_weights(B, False)

            def pool_h(m, j):
                for c in range(GC):
                    wait(pool, F["us"], GC * m + c + 1)
                    wait(pool, F["silu"], GC * m + c + 1)
                    if c == 0:
                        wait(pool, F["hsub"], m - 1)
                    pool.tensor_tensor(H1[j][:, c * GW_:(c + 1) * GW_], SL[c % 2][:, :], US[c % 2][:, :], ALU.mult) \
                        .then_inc(F["h"], 1)

            def pool_add(n, j):
                wait(pool, F["y"], n + 1)
                xs = X[:, n, :] if isinstance(n, int) else X[:, bass.ds(n, 1), :].rearrange("p a d -> p (a d)")
                pool.tensor_tensor(xs, xs, Y2[j][:, :], ALU.add).then_inc(F["res"], 1)

            pool_h(0, 0)
            with pool.Fori(0, B // 2 - 1) as p:
                pool_h(2 * p + 1, 1)
                pool_add(2 * p, 0)
                pool_h(2 * p + 2, 0)
                pool_add(2 * p + 1, 1)
            pool_h(B - 1, 1)
            pool_add(B - 2, 0)
            pool_add(B - 1, 1)

        NCH = len(FC)

        def act_gu(act, e, half):
            for c in range(NCH):
                step, par = NCH * (2 * e + half) + c, (half + c) % 2
                r = slice(0, FC[c])
                wait(act, E["gps"], step + 1)
                wait(act, E["hmul"], step - 1)
                act.activation(silu[r, par, :], PS[r, par, 0:HALF], ACT.Silu).then_inc(E["silu"], 1)
            for c in range(NCH):
                step, par = NCH * (2 * e + half) + c, (half + c) % 2
                r = slice(0, FC[c])
                wait(act, E["hmul"], step + 1)
                if c == 0:
                    wait(act, E["yps"], 4 * (2 * e + half - 1))
                act.copy(HH[r, c, half * HALF:(half + 1) * HALF], h32[r, par, :]).then_inc(E["hhi"], 1)

        def act_attn0_exp(act, n, j):
            for i in range(HG):
                wait(act, A["sub"], HG * n + i + 1)
                act.activation(P0[j][:, i, :, :], P0[j][:, i, :, :], ACT.Exp, scale=INV0).then_inc(A["exp"], 1)

        def act_attn0_q(act, p):
            for m in range(MT0):
                wait(act, A["qk"], 2 * MT0 * p + 2 * m + 1)
                if m == 0:
                    wait(act, A["sc"], 2 * HG * p)
                act.copy(QT[:, m, :, :], PS[:, 6, 0:2 * T].rearrange("p (b t) -> p b t", b=2)).then_inc(A["qsb"], 1)

        def act_attn0_tail(act, n):
            for i in range(HG):
                wait(act, A["pt"], (HG + 0) * n + i + 1)
                if i == 0:
                    wait(act, A["pv"], 2 * n)
                act.copy(PT[:, i, :, :], TP[i % 2][0:T]).then_inc(A["ptsb"], 1)
            wait(act, A["ot"], n + 1)
            wait(act, A["op"], n)
            act.copy(OH[:, :, :], TP[0]).then_inc(A["oh"], 1)

        def act_fold_m(act, i, j):
            wait(act, C["m"], i + 1)
            wait(act, C["nf"], i - 1)
            act.copy(m_sb[j][:, :, :], PS[:, j, 0:2 * R1].rearrange("p (h r) -> p h r", h=2)).then_inc(C["msb"], 1)

        def fold_cols(t, i):
            return t[:, :, i * 128:(i + 1) * 128] if isinstance(i, int) else t[:, :, bass.ds(i * 128, 128)]

        def act_fold_n(act, i, j):
            wait(act, C["nf"], i + 1)
            act.copy(fold_cols(NFH, i), PS[:, 2 + j, :].rearrange("p (k n) -> p k n", k=KC)).then_inc(C["nfh"], 1)

        def queries_part(k, hi):
            if k < 4:
                o = (QRH if hi else QRL)[:, 2 * k:2 * k + 2, :]
                return o, PS[:, k % 4, 0:4 * T].rearrange("p (m t) -> p m t", m=2)
            h0 = (k - 4) // 2 * 4 + k % 2
            o = (QH if hi else QL)[:, :, :].rearrange("p j (h t) -> p h j t", t=T)[:, h0:h0 + 3:2]
            return o, PS[:, k % 4, 0:4 * T].rearrange("p (h j t) -> p h j t", h=2, j=2)

        def act_queries(act, q, k):
            wait(act, C["pr"], 12 * q + k + 1)
            o, bank = queries_part(k, True)
            act.copy(o, bank).then_inc(C["prh"], 1)

        def turned(t):
            return PS[:, 4 + t % 3, 0:LK * 128].rearrange("p (c r) -> p c r", c=LK)[:, :, 0:tile_rows(t)]

        def pt_buffer(g, j):
            return 2 if g == NG - 1 else (g + j * (NG - 1)) % 2

        def pt_free(m, g):
            return NG * m if g == NG - 1 else NG * m + g - 1 if g >= 2 else NG * (m - 1) + g + 2

        def pt_place(buf, t, j):
            return buf[pt_buffer(t // 4, j)][:, :, t % 4 * 128:t % 4 * 128 + tile_rows(t)]

        def act_keys(act, n, j):
            wait(act, C["ktp"], n + 1)
            act.copy(KTH[j][:, :], PS[:, KBANK, 0:NKE]).then_inc(C["kth"], 1)
            wait(act, C["pv"], NG * (n - 1))
            wait(act, C["kvr"], n + 1)
            act.copy(KNH[j][:, :, :], kvr[:, :, :]).then_inc(C["knh"], 1)

        def act_steps(act, kind, n, j, q=None):
            for what, dn, t in attention_steps(kind):
                m, jj = (n, j) if dn == 0 else (n + dn, 1 - j)
                if what == "S":
                    r = slice(0, tile_rows(t))
                    wait(act, C["max"], RT * m + t + 1)
                    wait(act, C["pt"], RT * m + earlier(t, 8) + 1)
                    act.activation(P1[t % 8][r, 0:NK], PS[r, t % 4, 0:NK], ACT.Exp, bias=nmx[r, jj, t:t + 1],
                                   accum_out=rsum[r, jj, t:t + 1]).then_inc(C["exp"], 1)
                elif what == "PT":
                    wait(act, C["pt"], RT * m + t + 1)
                    if t % 4 == 0:
                        wait(act, C["pv"], pt_free(m, t // 4))
                    act.copy(pt_place(PTH, t, jj), turned(t)).then_inc(C["pth"], 1)
                elif what == "KV":
                    act_keys(act, n + 1, 1 - j)
                elif what == "PR":
                    act_queries(act, q, t)

        @block.scalar
        def _(act):
            for k, (a, z, name) in enumerate(SPLITS[:2]):
                act.wait_ge(A[name], 16)
                act.copy(hi0[:, a:z], raw0[:, a:z]).then_inc(A["whi"], 1)
            ln_act(act)
            for b in range(B):
                ln_high(act, 0, b, XH)
                if b == 1:
                    for a, z, name in SPLITS[2:]:
                        act.wait_ge(A[name], 16)
                        act.copy(hi0[:, a:z], raw0[:, a:z]).then_inc(A["whi"], 1)
            act.wait_ge(A["vones"], 1)
            for b in range(B):
                act.wait_ge(A["vps"], b + 1)
                act.copy(V[:, b, :, 0:HD0], PS[0:T, b % 2, :].rearrange("p (h d) -> p h d", h=NH0)).then_inc(A["vsb"], 1)
            act_attn0_q(act, 0)
            act_attn0_exp(act, 0, 0)
            with act.Fori(0, B // 2 - 1) as p:
                act_attn0_exp(act, 2 * p + 1, 1)
                act_attn0_q(act, p + 1)
                act_attn0_tail(act, 2 * p)
                act_attn0_exp(act, 2 * p + 2, 0)
                act_attn0_tail(act, 2 * p + 1)
            act_attn0_exp(act, B - 1, 1)
            act_attn0_tail(act, B - 2)
            act_attn0_tail(act, B - 1)
            lne_act(act)
            act.wait_ge(E["consts"], 32)
            act.copy(wg[1][:, :, :], wg[0][:, :, :]).then_inc(E["wghi"], 1)
            for b in range(B):
                ln_high(act, 1, b, XHB)
            act.wait_ge(E["diff"], 1)
            act.activation(gd[:, 1, :], gd[:, 0, :], ACT.Exp).then_inc(E["ex"], 1)
            act_gu(act, 0, 0)
            with act.Fori(0, NE // 2 - 1) as i:
                act_gu(act, 2 * i, 1)
                act_gu(act, 2 * i + 1, 0)
                act_gu(act, 2 * i + 1, 1)
                act_gu(act, 2 * i + 2, 0)
            act_gu(act, NE - 2, 1)
            act_gu(act, NE - 1, 0)
            act_gu(act, NE - 1, 1)
            lnc_act(act)
            act.wait_ge(C["kr"], 16)
            act.copy(WKH[:, :, :], kr_raw[:, :, :]).then_inc(C["krh"], 1)
            act_fold_m(act, 0, 0)
            with act.Fori(0, NP1 // 2 - 1) as i:
                act_fold_m(act, 2 * i + 1, 1)
                act_fold_n(act, 2 * i, 0)
                act_fold_m(act, 2 * i + 2, 0)
                act_fold_n(act, 2 * i + 1, 1)
            act_fold_m(act, NP1 - 1, 1)
            act_fold_n(act, NP1 - 2, 0)
            act_fold_n(act, NP1 - 1, 1)
            for b in range(B):
                ln_high(act, 2, b, XHC)
            act_keys(act, 0, 0)
            for k in range(12):
                act_queries(act, 0, k)
            act_steps(act, "even", 0, 0)
            with act.Fori(0, B // 2 - 1) as p:
                act_steps(act, "odd", 2 * p + 1, 1, p + 1)
                act_steps(act, "even", 2 * p + 2, 0)
            act_steps(act, "last", B - 1, 1)
            for h in range(NH0):
                act.wait_ge(O["pf"], h + 1)
                act.copy(PFH[:, h, :], PS[:, h % 4, :]).then_inc(O["pfh"], 1)

            def split_ctx(n, j):
                wait(act, O[f"cx{j}"], 8 * n + 16 - 8 * j)
                wait(act, O["out"], n - 1)
                act.copy(CXH[j][:, :], CXR[j][:, :]).then_inc(O["cxh"], 1)

            def act_weights(n, odd, p=None):
                tiles = wtiles(n if p is None else (p,), odd)
                for i, (kind, _) in enumerate(tiles):
                    wait(act, W["inv"], 3 * n + i + 1)
                    raw = WRT[i][:, 0:D] if kind == "up" else WRT[i]
                    act.activation(raw, raw, ACT.Identity, bias=mgc[:, 0:1], scale=wsc[i][:, 2:3]).then_inc(W["mag"], 1)
                for i, (kind, at) in enumerate(tiles):
                    wait(act, W["tr"], 3 * n + i + 1)
                    o, ch = (W1Q, KC) if kind == "up" else (W2Q, IC)
                    act.copy(o[:, :, cols_at(at, 128)], wbank(i, ch)).then_inc(W["ev"], 1)

            act.wait_ge(W["mgc"], 1)
            split_ctx(0, 0)
            with act.Fori(0, B // 2 - 1) as p:
                split_ctx(2 * p + 1, 1)
                act_weights(2 * p, False, p)
                split_ctx(2 * p + 2, 0)
                act_weights(2 * p + 1, True, p)
            split_ctx(B - 1, 1)
            act_weights(B - 2, False)
            act_weights(B - 1, True)
            act_weights(B, False)

            lnf_act(act)

            def act_xq(m, j):
                wait(act, F["inv"], m + 1)
                wait(act, F["sub"], m - 1)
                act.activation(XM[j][:, :], xn[:, j, :], ACT.Identity, bias=mgc[0:T, 0:1], scale=sx[:, j, 2:3]) \
                    .then_inc(F["mag"], 1)
                wait(act, F["xt"], m + 1)
                act.copy(XQT[j][:, :, :], PS[:, 6 + j, :].bitcast(BF16)[:, 0:KC * T].rearrange("p (k t) -> p k t", k=KC)) \
                    .then_inc(F["xev"], 1)

            def act_silu(m, c):
                wait(act, F["gs"], GC * m + c + 1)
                wait(act, F["h"], GC * m + c - 1)
                act.activation(SL[c % 2][:, :], GS[c % 2][:, :], ACT.Silu).then_inc(F["silu"], 1)

            def act_hq(n, j):
                wait(act, F["hinv"], n + 1)
                act.activation(H1[j][:, :], H1[j][:, :], ACT.Identity, bias=mgc[0:T, 0:1], scale=sh[:, j, 2:3]) \
                    .then_inc(F["hmag"], 1)

            def act_hev(n, j):
                for g, (a, z) in enumerate(HTG):
                    wait(act, F["ht"], 2 * n + g + 1)
                    act.copy(HQT[j][:, a:z, :], PS[:, 4 + g, :].bitcast(BF16)[:, 0:(z - a) * T]
                             .rearrange("p (k t) -> p k t", k=z - a)).then_inc(F["hev"], 1)

            def act_ffn(n, j):
                act_xq(n + 1, 1 - j)
                act_hq(n, j)
                act_silu(n + 1, 0)
                act_silu(n + 1, 1)
                act_hev(n, j)
                act_silu(n + 1, 2)
                act_silu(n + 1, 3)

            act_xq(0, 0)
            for c in range(GC):
                act_silu(0, c)
            with act.Fori(0, B // 2 - 1) as p:
                act_ffn(2 * p, 0)
                act_ffn(2 * p + 1, 1)
            act_ffn(B - 2, 0)
            act_hq(B - 1, 1)
            act_hev(B - 1, 1)

        def pe_gu(pe, e, half, j):
            t = slice(half * HALF, (half + 1) * HALF)
            wait(pe, E["lo12"], e + 1)
            for c in range(NCH):
                step, par = NCH * (2 * e + half) + c, (half + c) % 2
                for which, free, done in ((0, "silu", "gps"), (1, "hmul", "ups")):
                    wait(pe, E[free], step - 1)
                    for k in range(KC):
                        last = mm3(pe, PS[0:FC[c], 2 * which + par, 0:HALF], w12_of(wh[j], which, k, c),
                                   w12_of(wl[j], which, k, c), XHB[:, k, t], XLB[:, k, t], k == 0, k == KC - 1)
                    last.then_inc(E[done], 1)

        def pe_y(pe, e, half, j):
            u = 2 * e + half
            wait(pe, E["lo3"], e + 1)
            wait(pe, E["hlo"], NCH * (u + 1))
            for q in range(B // 2):
                wait(pe, E["yacc"], B // 2 * (u - 1) + q + 1)
                t = slice((half * 4 + q) * T, (half * 4 + q + 1) * T)
                for c in range(NCH):
                    r = slice(0, FC[c])
                    last = mm3(pe, PS[0:T, 4 + q, :], HH[r, c, t], HL[r, c, t], w3_of(wh[j], c), w3_of(wl[j], c),
                               c == 0, c == NCH - 1)
                last.then_inc(E["yps"], 1)

        def pe_attn0_qk(pe, p):
            if isinstance(p, int):
                xh, xl = XH[:, :, p * 2 * T:(p + 1) * 2 * T], XL[:, :, p * 2 * T:(p + 1) * 2 * T]
            else:
                xh, xl = XH[:, :, bass.ds(p * (2 * T), 2 * T)], XL[:, :, bass.ds(p * (2 * T), 2 * T)]
            for m in range(MT0):
                wait(pe, A["qsb"], MT0 * p + m)
                if m == 0:
                    wait(pe, A["onorm"], 4 * p - 4)
                for k in range(KC):
                    last = mm3(pe, PS[:, 6, 0:2 * T], wqh[:, k, m * 128:(m + 1) * 128], wql[:, k, m * 128:(m + 1) * 128],
                               xh[:, k], xl[:, k], k == 0, k == KC - 1)
                last.then_inc(A["qk"], 1)
                wait(pe, A["ksb"], MT0 * p + m)
                if isinstance(p, int):
                    ch, cl = cxh[:, 2 * p:2 * p + 2, :], cxl[:, 2 * p:2 * p + 2, :]
                else:
                    ch, cl = cxh[:, bass.ds(p * 2, 2), :], cxl[:, bass.ds(p * 2, 2), :]
                mm3(pe, PS[:, 7, 0:2 * T], wkvh[:, m * 128:(m + 1) * 128], wkvl[:, m * 128:(m + 1) * 128],
                    ch.rearrange("p b t -> p (b t)"), cl.rearrange("p b t -> p (b t)"), True, True).then_inc(A["qk"], 1)

        def pe_attn0_scores(pe, n, j):
            for i in range(HG):
                wait(pe, A["sub"], HG * (n - 1) + i + 1)
                pe.matmul(S0[i], identb[0:T, 0:T], maskb[:, None, :].broadcast_to((T, MT0, T)), start=True, stop=False)
            if j == 0:
                p = n // 2 if isinstance(n, int) else None
            wait(pe, A["qsb"], 2 * n + 4 - 2 * j)
            wait(pe, A["ksb"], 2 * n + 4 - 2 * j)
            for m in range(MT0):
                for i in range(HG):
                    r = slice(i * HD0, (i + 1) * HD0)
                    last = pe.matmul(S0[i][:, m, :], QT[r, m, j, :], KT[r, m, j, :], start=False, stop=(m == MT0 - 1),
                                     tile_position=(i * HD0, 0))
                    if m == MT0 - 1:
                        last.then_inc(A["sc"], 1)

        def pe_attn0_tail(pe, n, j):
            for i in range(HG):
                wait(pe, A["exp"], HG * n + i + 1)
                if i == 0:
                    wait(pe, A["ol"], n)
                elif i == 1:
                    wait(pe, A["res"], n)
                else:
                    wait(pe, A["ptsb"], HG * n + i - 1)
                for m in range(MT0):
                    last = pe.transpose(TP[i % 2][0:T, m, :], P0[j][:, i, m, :], ident[0:T, 0:T])
                last.then_inc(A["pt"], 1)
            nn = n if isinstance(n, int) else bass.ds(n, 1)
            if j == 0 and not (isinstance(n, int) and n == B - 2):
                wait(pe, A["qsb"], 2 * n + 2 * MT0)
                wait(pe, A["ksb"], 2 * n + 2 * MT0)
            for g in range(2):
                wait(pe, A["onorm"], 2 * (n - 1) + g + 1)
                for i in (2 * g, 2 * g + 1):
                    wait(pe, A["ptsb"], HG * n + i + 1)
                    for m in range(MT0):
                        v = V[:, n, m * HG + i, :] if isinstance(n, int) else \
                            V[:, bass.ds(n, 1), m * HG + i, :].rearrange("p a d -> p (a d)")
                        last = pe.matmul(OV[g][:, i % 2, m, :], PT[:, i, m, :], v, start=True, stop=True)
                last.then_inc(A["pv"], 1)
            wait(pe, A["onorm"], 2 * n + 2)
            for k in range(KC):
                last = pe.transpose(TP[0][:, k, :], O0[:, k * 128:(k + 1) * 128], ident[0:T, 0:T])
            last.then_inc(A["ot"], 1)
            wait(pe, A["ol"], n + 1)
            for k in range(KC):
                last = mm3(pe, PS[0:T, 5, :], OH[:, k, :], OL[:, k, :], woh[:, k, :], wol[:, k, :], k == 0, k == KC - 1)
            last.then_inc(A["op"], 1)

        def pe_fold_m(pe, i, j):
            wait(pe, C[f"fq{j}"], 8 * i + 16 - 8 * j)
            wait(pe, C["msb"], i - 1)
            for h in range(2):
                for c in range(LK):
                    last = pe.matmul(PS[:, j, h * R1:(h + 1) * R1], FQR[j][:, h, c * DK:(c + 1) * DK],
                                     FQR[j][:, h, CQ + c * R1:CQ + (c + 1) * R1], start=(c == 0), stop=(c == LK - 1))
            last.then_inc(C["m"], 1)

        def pe_fold_n(pe, i, j):
            wait(pe, C["msb"], i + 1)
            wait(pe, C["nfl"], i - 1)
            at = CQ + LK * R1
            for k in range(KC):
                for h in range(2):
                    last = pe.matmul(PS[:, 2 + j, k * 128 + h * R1:k * 128 + (h + 1) * R1],
                                     FQR[j][:, h, at + k * 128:at + (k + 1) * 128], m_sb[j][:, h, :], start=True, stop=True)
            last.then_inc(C["nf"], 1)

        def pe_queries(pe, q, k, n=None):
            bank = PS[:, k % 4, :]
            if n is not None and k < 4:
                wait(pe, C["exp"], RT * n + earlier(k, 4) + RT + 1)
            elif k >= 4:
                wait(pe, C["prl"], 12 * q + k - 3)
            if k < 4:
                for m in (2 * k, 2 * k + 1):
                    for c in range(KC):
                        if isinstance(q, int):
                            xh, xl = (t[:, c, q * 2 * T:(q + 1) * 2 * T] for t in (XHC, XLC))
                        else:
                            xh, xl = (t[:, c, bass.ds(q * (2 * T), 2 * T)] for t in (XHC, XLC))
                        last = mm3(pe, bank[:, m % 2 * 2 * T:(m % 2 + 1) * 2 * T], NFH[:, c, m * 128:(m + 1) * 128],
                                   NFL[:, c, m * 128:(m + 1) * 128], xh, xl, c == 0, c == KC - 1)
            else:
                c = k - 4
                wait(pe, C["prl"], 12 * q + c // 2 + 1)
                r = slice(c % 2 * R1, (c % 2 + 1) * R1)
                for h in range(2):
                    m = c // 2 * 2 + h
                    last = mm3(pe, bank[:, h * 2 * T:(h + 1) * 2 * T], WKH[r, m, :], WKL[r, m, :], QRH[r, m, :], QRL[r, m, :],
                               True, True)
            last.then_inc(C["pr"], 1)

        def pe_keys(pe, n, j):
            wait(pe, C["kvr"], n + 1)
            wait(pe, C["ptl"], RT * (n - 1) + KVAT - LAG - 2)
            for c in range(LK):
                last = pe.transpose(PS[:, KBANK, c * 128:(c + 1) * 128], kvr[:, c, :], ident[:, :])
            last.then_inc(C["ktp"], 1)

        def pe_steps(pe, kind, n, j, q=None):
            for what, dn, t in attention_steps(kind):
                m, jj = (n, j) if dn == 0 else (n + dn, 1 - j)
                r = tile_rows(t)
                if what == "S":
                    wait(pe, C["exp"], RT * m + earlier(t, 4) + 1)
                    if t < 4:
                        wait(pe, C["prl"], 6 * m + 12 - 6 * jj)
                        wait(pe, C["ktl"], m + 1)
                    c = slice(t * 128, t * 128 + r)
                    mm3(pe, PS[0:r, t % 4, 0:NKE], QH[:, jj, c], QL[:, jj, c], KTH[jj][:, :], KTL[jj][:, :], True, True) \
                        .then_inc(C["s"], 1)
                elif what == "PT":
                    wait(pe, C["nrm"], RT * m + t + 1)
                    wait(pe, C["ptl"], RT * m + earlier(t, 3) + 1)
                    if dn == 0 and t == KVAT - LAG and kind != "last":
                        wait(pe, C["ktl"], m + 2)
                    for c in range(LK):
                        last = pe.transpose(PS[:, 4 + t % 3, c * 128:(c + 1) * 128], P1[t % 8][:, c * 128:(c + 1) * 128],
                                            ident[:, :])
                    last.then_inc(C["pt"], 1)
                elif what == "PV":
                    g, c = divmod(t, LK)
                    cols = min(512, ROWS - g * 512)
                    if c == 0:
                        wait(pe, C["ptl"], RT * m + min(4 * g + 4, RT))
                        wait(pe, C["ctxo"], NG * m + g)
                        wait(pe, C["knl"], m + 1)
                    last = mm3(pe, PS[:, 7, 0:cols], KNH[jj][:, c, :], KNL[jj][:, c, :],
                               PTH[pt_buffer(g, jj)][:, c, 0:cols], PTL[pt_buffer(g, jj)][:, c, 0:cols], c == 0, c == LK - 1)
                    if c == LK - 1:
                        last.then_inc(C["pv"], 1)
                elif what == "KV":
                    pe_keys(pe, n + 1, 1 - j)
                else:
                    pe_queries(pe, q, t, n)

        @block.tensor
        def _(pe):
            pe.wait_ge(A["consts"], 32)
            for b in range(B):
                ln_transposes(pe, 0, b)
            pe.wait_ge(A["wlo"], 2)
            for b in range(B):
                wait(pe, A["vsb"], b - 1)
                mm3(pe, PS[0:T, b % 2, :], cxh[:, b, :], cxl[:, b, :], wkvh[:, D:2 * D], wkvl[:, D:2 * D], True, True) \
                    .then_inc(A["vps"], 1)
            pe.wait_ge(A["wlo"], 4)
            pe.wait_ge(LN["lo"], B)
            pe.wait_ge(A["cast"], 2)
            pe_attn0_qk(pe, 0)
            pe.wait_ge(A["vsb"], B)
            pe_attn0_scores(pe, 0, 0)
            with pe.Fori(0, B // 2 - 1) as p:
                pe_attn0_scores(pe, 2 * p + 1, 1)
                pe_attn0_qk(pe, p + 1)
                pe_attn0_tail(pe, 2 * p, 0)
                pe_attn0_scores(pe, 2 * p + 2, 0)
                pe_attn0_tail(pe, 2 * p + 1, 1)
            pe_attn0_scores(pe, B - 1, 1)
            pe_attn0_tail(pe, B - 2, 0)
            pe_attn0_tail(pe, B - 1, 1)
            pe.wait_ge(E["wglo"], 1)
            for b in range(B + 1):
                if b < B:
                    ln_transposes(pe, 1, b)
                if b > 0:
                    pe.wait_ge(LN["lo"], B + b)
                    t = slice((b - 1) * T, b * T)
                    for k in range(KC):
                        last = mm3(pe, PS[0:T, 6, (b - 1) * NE:b * NE], XHB[:, k, t], XLB[:, k, t], wg[1][:, k], wg[2][:, k],
                                   k == 0, k == KC - 1)
                    last.then_inc(E["gate"], 1)
            pe.wait_ge(E["logits"], 1)
            pe_gu(pe, 0, 0, 0)
            with pe.Fori(0, NE // 2 - 1) as i:
                pe_gu(pe, 2 * i, 1, 0)
                pe_y(pe, 2 * i, 0, 0)
                pe_gu(pe, 2 * i + 1, 0, 1)
                pe_y(pe, 2 * i, 1, 0)
                pe_gu(pe, 2 * i + 1, 1, 1)
                pe_y(pe, 2 * i + 1, 0, 1)
                pe_gu(pe, 2 * i + 2, 0, 0)
                pe_y(pe, 2 * i + 1, 1, 1)
            pe_gu(pe, NE - 2, 1, 0)
            pe_y(pe, NE - 2, 0, 0)
            pe_gu(pe, NE - 1, 0, 1)
            pe_y(pe, NE - 2, 1, 0)
            pe_gu(pe, NE - 1, 1, 1)
            pe_y(pe, NE - 1, 0, 1)
            pe_y(pe, NE - 1, 1, 1)
            pe_fold_m(pe, 0, 0)
            with pe.Fori(0, NP1 // 2 - 1) as i:
                pe_fold_m(pe, 2 * i + 1, 1)
                pe_fold_n(pe, 2 * i, 0)
                pe_fold_m(pe, 2 * i + 2, 0)
                pe_fold_n(pe, 2 * i + 1, 1)
            pe_fold_m(pe, NP1 - 1, 1)
            pe_fold_n(pe, NP1 - 2, 0)
            pe_fold_n(pe, NP1 - 1, 1)
            for b in range(B):
                ln_transposes(pe, 2, b)
            pe.wait_ge(LN["lo"], 3 * B)
            pe_keys(pe, 0, 0)
            pe.wait_ge(C["nfl"], NP1)
            pe.wait_ge(C["krl"], 1)
            for k in range(12):
                pe_queries(pe, 0, k)
            pe_steps(pe, "even", 0, 0)
            with pe.Fori(0, B // 2 - 1) as p:
                pe_steps(pe, "odd", 2 * p + 1, 1, p + 1)
                pe_steps(pe, "even", 2 * p + 2, 0)
            pe_steps(pe, "last", B - 1, 1)
            for h in range(NH0):
                i, j = h // 2, h // 2 % 2
                if h % 2 == 0:
                    pe.wait_ge(O[f"fp{j}"], 16 * (i // 2 + 1))
                wait(pe, O["pfl"], h - 3)
                pe.matmul(PS[:, h % 4, :], FPR[j][:, h % 2, 0:DK], FPR[j][:, h % 2, DK:FP], start=True, stop=True) \
                    .then_inc(O["pf"], 1)

            def project(n, j):
                wait(pe, O["cxl"], n + 1)
                wait(pe, O["res"], n - 1)
                for h in range(NH0):
                    t = slice(h * T, (h + 1) * T)
                    last = mm3(pe, PS[0:T, 4 + j, :], CXH[j][:, t], CXL[j][:, t], PFH[:, h, :], PFL[:, h, :], h == 0, h == NH0 - 1)
                last.then_inc(O["out"], 1)

            pe.wait_ge(O["pfl"], NH0)
            def pe_weights(n, odd, p=None):
                for i, (kind, _) in enumerate(wtiles(n if p is None else (p,), odd)):
                    wait(pe, W["sub"], 3 * n + i + 1)
                    wait(pe, W["ev"], 3 * (n - 1) + i + 1)
                    ch = KC if kind == "up" else IC
                    for c in range(ch):
                        last = pe.transpose(wbank(i, ch)[:, c, :], WQT[i][:, c * 128:(c + 1) * 128], identb[:, :])
                    last.then_inc(W["tr"], 1)
                    wait(pe, W["dg"], 3 * n + i + 1)
                    wait(pe, W["sb"], 3 * (n - 2) + 3)
                    pe.matmul(PS[0:T, 6 + odd, i * 128:(i + 1) * 128], ones[:, :], diag[i][:, :], start=True, stop=True) \
                        .then_inc(W["bc"], 1)

            pe.wait_ge(W["ones"], 1)
            with pe.Fori(0, B // 2) as p:
                project(2 * p, 0)
                pe_weights(2 * p, 0, p)
                project(2 * p + 1, 1)
                pe_weights(2 * p + 1, 1, p)
            pe_weights(B, 0)

            def pe_xq(m, j):
                wait(pe, F["sub"], m + 1)
                if isinstance(m, int) and m == 0:
                    pe.wait_ge(W["sb"], UT + DT)
                wait(pe, F["y"], m - 1)
                for k in range(KC):
                    last = pe.transpose(PS[:, 6 + j, :].bitcast(BF16)[:, k * T:(k + 1) * T], XQ[j][:, k * 128:(k + 1) * 128],
                                        identb[0:T, 0:T])
                last.then_inc(F["xt"], 1)

            def pe_gate_up(m, j, c):
                if c == 0:
                    wait(pe, F["xev"], m + 1)
                for which, free, done in ((0, "gs", "gps"), (1, "us", "ups")):
                    wait(pe, F[free], GC * m + c - 1)
                    at = which * FI + c * GW_
                    for k in range(KC):
                        last = pe.matmul(PS[0:T, 2 * which + c % 2, 0:GW_], XQT[j][:, k, :], W1Q[:, k, at:at + GW_],
                                         start=(k == 0), stop=(k == KC - 1))
                    last.then_inc(F[done], 1)

            def pe_ht(n, j):
                wait(pe, F["hsub"], n + 1)
                for g, (a, z) in enumerate(HTG):
                    wait(pe, F["hev"], 2 * (n - 1) + g + 1)
                    for c in range(a, z):
                        last = pe.transpose(PS[:, 4 + g, :].bitcast(BF16)[:, (c - a) * T:(c - a + 1) * T],
                                            HQ[j][:, c * 128:(c + 1) * 128], identb[0:T, 0:T])
                    last.then_inc(F["ht"], 1)

            def pe_down(n, j):
                wait(pe, F["hev"], 2 * n + 2)
                for c in range(IC):
                    last = pe.matmul(PS[0:T, 6 + j, :], HQT[j][:, c, :], W2Q[:, c, :], start=(c == 0), stop=(c == IC - 1))
                last.then_inc(F["dn"], 1)

            def pe_ffn(n, j):
                pe_xq(n + 1, 1 - j)
                pe_gate_up(n + 1, 1 - j, 0)
                pe_gate_up(n + 1, 1 - j, 1)
                pe_ht(n, j)
                pe_gate_up(n + 1, 1 - j, 2)
                pe_gate_up(n + 1, 1 - j, 3)
                pe_down(n, j)

            pe_xq(0, 0)
            pe.wait_ge(W["ev"], UT + DT)
            for c in range(GC):
                pe_gate_up(0, 0, c)
            with pe.Fori(0, B // 2 - 1) as p:
                pe_ffn(2 * p, 0)
                pe_ffn(2 * p + 1, 1)
            pe_ffn(B - 2, 0)
            pe_ht(B - 1, 1)
            pe_down(B - 1, 1)

        def dve_gu(dve, e, half):
            for c in range(NCH):
                step, par = NCH * (2 * e + half) + c, (half + c) % 2
                r = slice(0, FC[c])
                wait(dve, E["ups"], step + 1)
                wait(dve, E["silu"], step + 1)
                wait(dve, E["hlo"], step - 1)
                dve.tensor_tensor(h32[r, par, :], silu[r, par, :], PS[r, 2 + par, 0:HALF], ALU.mult).then_inc(E["hmul"], 1)
                if c > 0:
                    dve_hlow(dve, e, half, c - 1)
            dve_hlow(dve, e, half, NCH - 1)

        def dve_hlow(dve, e, half, c):
            step, par = NCH * (2 * e + half) + c, (half + c) % 2
            r, t = slice(0, FC[c]), slice(half * HALF, (half + 1) * HALF)
            wait(dve, E["hhi"], step + 1)
            dve.tensor_tensor(HL[r, c, t], h32[r, par, :], HH[r, c, t].bitcast(F32), ALU.subtract).then_inc(E["hlo"], 1)

        def dve_y(dve, e, half):
            u = 2 * e + half
            for q in range(B // 2):
                b = half * 4 + q
                wait(dve, E["yps"], B // 2 * u + q + 1)
                wait(dve, E["yacc"], B // 2 * (u - 2) + q + 1)
                w = GW[:, e, b:b + 1] if isinstance(e, int) else GW[:, bass.ds(e, 1), b]
                dve.scalar_tensor_tensor(X[:, b, :], PS[0:T, 4 + q, :], w, X[:, b, :], ALU.mult, ALU.add) \
                    .then_inc(E["yacc"], 1)

        def dve_hi12(dve, e, j):
            wait(dve, E["d12"], 16 * (e + 1))
            wait(dve, E["ups"], NCH * 2 * (e - 1))
            dve.tensor_copy(wh[j][:, 0:W12], wraw[:, 0:W12]).then_inc(E["hi12"], 1)

        def dve_hi3(dve, e, j):
            wait(dve, E["d3"], 32 * (e + 1))
            wait(dve, E["yps"], B * (e - 1))
            dve.tensor_copy(wh[j][:, W12:], wraw[:, W12:]).then_inc(E["hi3"], 1)

        def dve_gating(dve):
            dve.wait_ge(E["gate"], B)
            dve.tensor_copy(logits[:, :, :], PS[0:T, 6, 0:B * NE].rearrange("p (b e) -> p b e", b=B)).then_inc(E["logits"], 1)
            dve.wait_ge(E["logits"], 1)
            for b in range(B):
                dve.max(top8[:, b, :], logits[:, b, :]).then_inc(E["gating"], 1)
            dve.wait_ge(E["gating"], 8)
            for b in range(B):
                dve.max_index(top8i[:, b, :], top8[:, b, :], logits[:, b, :]).then_inc(E["gating"], 1)
            dve.tensor_tensor(gd[:, 0, :], top8[:, :, 1], top8[:, :, 0], ALU.subtract).then_inc(E["diff"], 1)
            dve.wait_ge(E["gating"], 16)
            dve.tensor_copy(top2i[:, :, :], top8i[:, :, 0:2]).then_inc(E["gating"], 1)
            dve.wait_ge(E["ex"], 1)
            dve.tensor_scalar(gd[:, 2, :], gd[:, 1, :], 1.0, None, ALU.add).then_inc(E["gating"], 1)
            dve.wait_ge(E["gating"], 18)
            dve.reciprocal(gd[:, 3, :], gd[:, 2, :]).then_inc(E["gating"], 1)
            dve.wait_ge(E["gating"], 19)
            dve.tensor_tensor(gd[:, 2, :], gd[:, 3, :], gd[:, 1, :], ALU.mult).then_inc(E["gating"], 1)
            dve.wait_ge(E["gating"], 17)
            dve.wait_ge(E["consts"], 32)
            for i in range(2):
                dve.tensor_tensor(geq[:, i, :, :], iota[:, None, :].broadcast_to((T, B, NE)),
                                  top2i[:, :, i, None].broadcast_to((T, B, NE)), ALU.is_equal).then_inc(E["gating"], 1)
            dve.wait_ge(E["gating"], 22)
            dve.wait_ge(E["gating"], 20)
            for i in range(2):
                dve.tensor_tensor(geq[:, 2 + i, :, :], geq[:, i, :, :],
                                  gd[:, 3 - i, :, None].broadcast_to((T, B, NE)), ALU.mult).then_inc(E["gating"], 1)
            dve.wait_ge(E["gating"], 24)
            dve.tensor_tensor(GW[:, :, :].rearrange("p e b -> p b e"), geq[:, 2, :, :], geq[:, 3, :, :], ALU.add) \
                .then_inc(E["gating"], 1)
            dve.wait_ge(E["gating"], 25)

        def dve_attn0_softmax(dve, n, j):
            wait(dve, A["pt"], HG * (n - 1))
            for i in range(HG):
                wait(dve, A["sc"], HG * n + i + 1)
                dve.tensor_reduce(mx0[:, j, i, :], S0[i], AX.X, ALU.max).then_inc(A["mx"], 1)
            for i in range(HG):
                wait(dve, A["mx"], HG * n + i + 1)
                dve.tensor_tensor(P0[j][:, i, :, :], S0[i], mx0[:, j, i, :, None].broadcast_to((T, MT0, T)),
                                  ALU.subtract).then_inc(A["sub"], 1)

        def dve_attn0_k(dve, p):
            for m in range(MT0):
                wait(dve, A["qk"], 2 * MT0 * p + 2 * m + 2)
                if m == 0:
                    wait(dve, A["sc"], 2 * HG * p)
                dve.tensor_copy(KT[:, m, :, :], PS[:, 7, 0:2 * T].rearrange("p (b t) -> p b t", b=2)).then_inc(A["ksb"], 1)

        def dve_attn0_tail(dve, n):
            ov = O0[:, :].rearrange("p (m i d) -> p i m d", m=MT0, i=HG)
            for g in range(2):
                wait(dve, A["pv"], 2 * n + g + 1)
                dve.reciprocal(rs0[:, 2 * g:2 * g + 2, :], OV[g][:, :, :, HD0]).then_inc(A["rs"], 1)
                wait(dve, A["rs"], 2 * n + g + 1)
                if g == 0:
                    wait(dve, A["ot"], n)
                for i in range(2):
                    x_ = dve.tensor_tensor(ov[:, 2 * g + i, :, :], OV[g][:, i, :, 0:HD0],
                                      rs0[:, 2 * g + i, :, None].broadcast_to((T, MT0, HD0)), ALU.mult)
                x_.then_inc(A["onorm"], 1)
            wait(dve, A["oh"], n + 1)
            dve.tensor_tensor(OL[:, :, :], TP[0], OH[:, :, :].bitcast(F32), ALU.subtract).then_inc(A["ol"], 1)
            wait(dve, A["op"], n + 1)
            xs = X[:, n, :] if isinstance(n, int) else X[:, bass.ds(n, 1), :].rearrange("p a d -> p (a d)")
            dve.tensor_tensor(xs, xs, PS[0:T, 5, :], ALU.add).then_inc(A["res"], 1)

        def dve_fold(dve, i, j):
            wait(dve, C["nfh"], i + 1)
            dve.tensor_tensor(fold_cols(NFL, i), PS[:, 2 + j, :].rearrange("p (k n) -> p k n", k=KC),
                              fold_cols(NFH, i).bitcast(F32), ALU.subtract).then_inc(C["nfl"], 1)

        def dve_queries(dve, q, k):
            wait(dve, C["prh"], 12 * q + k + 1)
            o, bank = queries_part(k, False)
            hi, _ = queries_part(k, True)
            if k < 4:
                dve.tensor_tensor(o, bank, hi.bitcast(F32), ALU.subtract).then_inc(C["prl"], 1)
            else:
                dve.tensor_tensor(o, bank, hi.bitcast(F32), ALU.subtract).then_inc(C["prl"], 1)

        def dve_keys(dve, n, j):
            wait(dve, C["kth"], n + 1)
            dve.tensor_tensor(KTL[j][:, :], PS[:, KBANK, 0:NKE], KTH[j][:, :].bitcast(F32), ALU.subtract).then_inc(C["ktl"], 1)

        def dve_steps(dve, kind, n, j, q=None):
            behind = []

            def invert(m, jj, t):
                r = slice(0, tile_rows(t))
                wait(dve, C["exp"], RT * m + t + 1)
                dve.reciprocal(rinv[r, jj, t:t + 1], rsum[r, jj, t:t + 1]).then_inc(C["inv"], 1)

            for what, dn, t in attention_steps(kind, vector=True):
                m, jj = (n, j) if dn == 0 else (n + dn, 1 - j)
                if what == "S":
                    r = slice(0, tile_rows(t))
                    wait(dve, C["s"], RT * m + t + 1)
                    dve.tensor_reduce(nmx[r, jj, t:t + 1], PS[r, t % 4, 0:NK], AX.X, ALU.max, negate=True).then_inc(C["max"], 1)
                elif what == "PT":
                    wait(dve, C["pth"], RT * m + t + 1)
                    dve.tensor_tensor(pt_place(PTL, t, jj), turned(t), pt_place(PTH, t, jj).bitcast(F32), ALU.subtract) \
                        .then_inc(C["ptl"], 1)
                elif what == "PV":
                    t, c = divmod(t, LK)
                    if c < LK - 1:
                        continue
                    cols = min(512, ROWS - t * 512)
                    wait(dve, C["pv"], NG * m + t + 1)
                    wait(dve, C[f"st{t % 2}"], 16 * (NG // 2) * m + 16 * (t // 2))
                    dve.tensor_copy(ctxo[t % 2][:, 0:cols], PS[:, 7, 0:cols]).then_inc(C["ctxo"], 1)
                elif what == "KV":
                    dve_keys(dve, n + 1, 1 - j)
                elif what == "PR":
                    dve_queries(dve, q, t)
                if behind:
                    invert(*behind.pop(0))
                if what == "S":
                    behind.append((m, jj, t))
            for rest in behind:
                invert(*rest)

        @block.vector
        def _(dve):
            dve.wait_ge(A["x"], 32)
            ln_vec(dve)

            def split(k):
                a, z, _ = SPLITS[k]
                dve.wait_ge(A["whi"], k + 1)
                dve.tensor_tensor(lo0[:, a:z], raw0[:, a:z], hi0[:, a:z].bitcast(F32), ALU.subtract).then_inc(A["wlo"], 1)

            normalise(dve, 0, 0)
            normalise(dve, 0, 1)
            split(0)
            split(1)
            for b in range(B):
                ln_low(dve, 0, b, XH, XL)
                if b + 2 < B:
                    normalise(dve, 0, b + 2)
            split(2)
            split(3)
            dve_attn0_k(dve, 0)
            dve_attn0_softmax(dve, 0, 0)
            with dve.Fori(0, B // 2 - 1) as p:
                dve_attn0_softmax(dve, 2 * p + 1, 1)
                dve_attn0_k(dve, p + 1)
                dve_attn0_tail(dve, 2 * p)
                dve_attn0_softmax(dve, 2 * p + 2, 0)
                dve_attn0_tail(dve, 2 * p + 1)
            dve_attn0_softmax(dve, B - 1, 1)
            dve_attn0_tail(dve, B - 2)
            dve_attn0_tail(dve, B - 1)
            dve.wait_ge(A["res"], B)
            lne_vec(dve)
            normalise(dve, 1, 0)
            normalise(dve, 1, 1)
            dve_hi12(dve, 0, 0)
            dve_hi3(dve, 0, 0)
            dve.wait_ge(E["wghi"], 1)
            dve.tensor_tensor(wg[2][:, :, :], wg[0][:, :, :], wg[1][:, :, :].bitcast(F32), ALU.subtract).then_inc(E["wglo"], 1)
            for b in range(B):
                ln_low(dve, 1, b, XHB, XLB)
                if b + 2 < B:
                    normalise(dve, 1, b + 2)
            dve_gating(dve)
            dve_gu(dve, 0, 0)
            with dve.Fori(0, NE // 2 - 1) as i:
                dve_hi12(dve, 2 * i + 1, 1)
                dve_gu(dve, 2 * i, 1)
                dve_y(dve, 2 * i, 0)
                dve_hi3(dve, 2 * i + 1, 1)
                dve_gu(dve, 2 * i + 1, 0)
                dve_y(dve, 2 * i, 1)
                dve_hi12(dve, 2 * i + 2, 0)
                dve_gu(dve, 2 * i + 1, 1)
                dve_y(dve, 2 * i + 1, 0)
                dve_hi3(dve, 2 * i + 2, 0)
                dve_gu(dve, 2 * i + 2, 0)
                dve_y(dve, 2 * i + 1, 1)
            dve_hi12(dve, NE - 1, 1)
            dve_gu(dve, NE - 2, 1)
            dve_y(dve, NE - 2, 0)
            dve_hi3(dve, NE - 1, 1)
            dve_gu(dve, NE - 1, 0)
            dve_y(dve, NE - 2, 1)
            dve_gu(dve, NE - 1, 1)
            dve_y(dve, NE - 1, 0)
            dve_y(dve, NE - 1, 1)
            dve.wait_ge(E["yacc"], B * NE)
            lnc_vec(dve)
            normalise(dve, 2, 0)
            normalise(dve, 2, 1)
            dve.wait_ge(C["krh"], 1)
            dve.tensor_tensor(WKL[:, :, :], kr_raw[:, :, :], WKH[:, :, :].bitcast(F32), ALU.subtract).then_inc(C["krl"], 1)
            with dve.Fori(0, NP1 // 2) as i:
                dve_fold(dve, 2 * i, 0)
                dve_fold(dve, 2 * i + 1, 1)
            for b in range(B):
                ln_low(dve, 2, b, XHC, XLC)
                if b + 2 < B:
                    normalise(dve, 2, b + 2)
            dve_keys(dve, 0, 0)
            for k in range(12):
                dve_queries(dve, 0, k)
            dve_steps(dve, "even", 0, 0)
            with dve.Fori(0, B // 2 - 1) as p:
                dve_steps(dve, "odd", 2 * p + 1, 1, p + 1)
                dve_steps(dve, "even", 2 * p + 2, 0)
            dve_steps(dve, "last", B - 1, 1)
            for h in range(NH0):
                dve.wait_ge(O["pfh"], h + 1)
                dve.tensor_tensor(PFL[:, h, :], PS[:, h % 4, :], PFH[:, h, :].bitcast(F32), ALU.subtract).then_inc(O["pfl"], 1)

            def low_ctx(n, j):
                wait(dve, O["cxh"], n + 1)
                dve.tensor_tensor(CXL[j][:, :], CXR[j][:, :], CXH[j][:, :].bitcast(F32), ALU.subtract).then_inc(O["cxl"], 1)

            def add_out(n, j):
                wait(dve, O["out"], n + 1)
                xs = X[:, n, :] if isinstance(n, int) else X[:, bass.ds(n, 1), :].rearrange("p a d -> p (a d)")
                dve.tensor_tensor(xs, xs, PS[0:T, 4 + j, :], ALU.add).then_inc(O["res"], 1)

            def dve_weights(n, odd, p=None):
                tiles = wtiles(n if p is None else (p,), odd)

                def quantise(i, kind):
                    wait(dve, W["mag"], 3 * n + i + 1)
                    wait(dve, W["tr"], 3 * (n - 1) + i + 1)
                    w = D if kind == "up" else FI
                    dve.tensor_scalar(WQT[i][:, 0:w], WRT[i][:, 0:w], MAGIC, None, ALU.subtract).then_inc(W["sub"], 1)

                for i, (kind, _) in enumerate(tiles):
                    w = D if kind == "up" else FI
                    wait(dve, W[f"ld{i}"], 16 * n + 16)
                    wait(dve, W["dg"], 3 * (n - 1) + i + 1)
                    dve.tensor_reduce(wsc[i][:, 0:1], WRT[i][:, 0:w], AX.X, ALU.max, apply_absolute_value=True).then_inc(W["max"], 1)
                    wait(dve, W["max"], 3 * n + i + 1)
                    dve.tensor_scalar(wsc[i][:, 1:2], wsc[i][:, 0:1], 1.0 / QMAX, QEPS, ALU.mult, ALU.max).then_inc(W["sc"], 1)
                    wait(dve, W["sc"], 3 * n + i + 1)
                    dve.reciprocal(wsc[i][:, 2:3], wsc[i][:, 1:2]).then_inc(W["inv"], 1)
                    if i > 0:
                        quantise(i - 1, tiles[i - 1][0])
                quantise(len(tiles) - 1, tiles[-1][0])

            def dve_scales(n, odd, p=None):
                tiles = wtiles(n if p is None else (p,), odd)
                wait(dve, W["bc"], 3 * n + len(tiles))
                ups = sum(kind == "up" for kind, _ in tiles)
                first = tiles[0][1] * 128
                o = S1B[:, first:first + ups * 128] if isinstance(first, int) else S1B[:, bass.ds(first, ups * 128)]
                dve.tensor_copy(o, PS[0:T, 6 + odd, 0:ups * 128]).then_inc(W["sb"], ups)
                if ups < len(tiles):
                    dve.tensor_copy(S2B[:, cols_at(tiles[-1][1], 128)], PS[0:T, 6 + odd, ups * 128:(ups + 1) * 128])                         .then_inc(W["sb"], 1)

            low_ctx(0, 0)
            with dve.Fori(0, B // 2 - 1) as p:
                low_ctx(2 * p + 1, 1)
                dve_weights(2 * p, 0, p)
                add_out(2 * p, 0)
                dve_scales(2 * p, 0, p)
                low_ctx(2 * p + 2, 0)
                dve_weights(2 * p + 1, 1, p)
                add_out(2 * p + 1, 1)
                dve_scales(2 * p + 1, 1, p)
            low_ctx(B - 1, 1)
            dve_weights(B - 2, 0)
            add_out(B - 2, 0)
            dve_scales(B - 2, 0)
            dve_weights(B - 1, 1)
            add_out(B - 1, 1)
            dve_scales(B - 1, 1)
            dve_weights(B, 0)
            dve_scales(B, 0)

            dve.wait_ge(O["res"], B)
            lnf_vec(dve)

            def dve_xq(m, j):
                xs = X[:, m, :] if isinstance(m, int) else X[:, bass.ds(m, 1), :].rearrange("p a d -> p (a d)")
                mean = mv[:, m, 0:1] if isinstance(m, int) else mv[:, bass.ds(m, 1), 0]
                r = rstd[:, m:m + 1] if isinstance(m, int) else rstd[:, bass.ds(m, 1)]
                wait(dve, F["mag"], m - 1)
                dve.tensor_scalar(xn[:, j, :], xs, mean, r, ALU.subtract, ALU.mult).then_inc(F["xn"], 1)
                wait(dve, F["xn"], m + 1)
                dve.tensor_reduce(sx[:, j, 0:1], xn[:, j, :], AX.X, ALU.max, apply_absolute_value=True).then_inc(F["xscale"], 1)
                wait(dve, F["xscale"], 2 * m + 1)
                dve.tensor_scalar(sx[:, j, 1:2], sx[:, j, 0:1], 1.0 / QMAX, QEPS, ALU.mult, ALU.max).then_inc(F["xscale"], 1)
                wait(dve, F["xscale"], 2 * m + 2)
                dve.reciprocal(sx[:, j, 2:3], sx[:, j, 1:2]).then_inc(F["inv"], 1)

            def dve_xsub(m, j):
                wait(dve, F["mag"], m + 1)
                wait(dve, F["xt"], m - 1)
                dve.tensor_scalar(XQ[j][:, :], XM[j][:, :], MAGIC, None, ALU.subtract).then_inc(F["sub"], 1)

            def dve_gate_up(m, j, c):
                at = c * GW_
                wait(dve, F["gps"], GC * m + c + 1)
                wait(dve, F["silu"], GC * m + c - 1)
                dve.scalar_tensor_tensor(GS[c % 2][:, :], PS[0:T, c % 2, 0:GW_], sx[:, j, 1:2], S1B[:, at:at + GW_],
                                         ALU.mult, ALU.mult).then_inc(F["gs"], 1)
                wait(dve, F["ups"], GC * m + c + 1)
                wait(dve, F["h"], GC * m + c - 1)
                dve.scalar_tensor_tensor(US[c % 2][:, :], PS[0:T, 2 + c % 2, 0:GW_], sx[:, j, 1:2], S1B[:, FI + at:FI + at + GW_],
                                         ALU.mult, ALU.mult).then_inc(F["us"], 1)

            def dve_hscale(n, j):
                wait(dve, F["h"], GC * (n + 1))
                dve.tensor_reduce(sh[:, j, 0:1], H1[j][:, :], AX.X, ALU.max, apply_absolute_value=True).then_inc(F["hscale"], 1)
                wait(dve, F["hscale"], 2 * n + 1)
                dve.tensor_scalar(sh[:, j, 1:2], sh[:, j, 0:1], 1.0 / QMAX, QEPS, ALU.mult, ALU.max).then_inc(F["hscale"], 1)
                wait(dve, F["hscale"], 2 * n + 2)
                dve.reciprocal(sh[:, j, 2:3], sh[:, j, 1:2]).then_inc(F["hinv"], 1)

            def dve_hsub(n, j):
                wait(dve, F["hmag"], n + 1)
                wait(dve, F["ht"], 2 * (n - 1))
                dve.tensor_scalar(HQ[j][:, :], H1[j][:, :], MAGIC, None, ALU.subtract).then_inc(F["hsub"], 1)

            def dve_out(n, j):
                wait(dve, F["dn"], n + 1)
                wait(dve, F["res"], n - 1)
                dve.scalar_tensor_tensor(Y2[j][:, :], PS[0:T, 6 + j, :], sh[:, j, 1:2], S2B[:, :],
                                         ALU.mult, ALU.mult).then_inc(F["y"], 1)

            def dve_ffn(n, j):
                dve_xq(n + 1, 1 - j)
                dve_hscale(n, j)
                dve_xsub(n + 1, 1 - j)
                dve_gate_up(n + 1, 1 - j, 0)
                dve_hsub(n, j)
                dve_gate_up(n + 1, 1 - j, 1)
                dve_gate_up(n + 1, 1 - j, 2)
                dve_gate_up(n + 1, 1 - j, 3)
                dve_out(n, j)

            dve_xq(0, 0)
            dve_xsub(0, 0)
            for c in range(GC):
                dve_gate_up(0, 0, c)
            with dve.Fori(0, B // 2 - 1) as p:
                dve_ffn(2 * p, 0)
                dve_ffn(2 * p + 1, 1)
            dve_ffn(B - 2, 0)
            dve_hscale(B - 1, 1)
            dve_hsub(B - 1, 1)
            dve_out(B - 1, 1)


def rope_tables():
    f = np.float32
    inv = (f(1.0) / f(10000.0) ** (np.arange(0, DK, 2, dtype=f) / f(DK))).astype(f)
    angle = (np.arange(NK, dtype=f)[:, None] * inv[None, :]).astype(f)
    cos, sin = (np.repeat(fn(angle), 2, axis=-1).astype(f) for fn in (np.cos, np.sin))
    sin[:, :DK // 2] *= -1

    def lay(t):
        rows = np.zeros((LK * 128, DK), f)
        rows[:NK] = t
        return rows.reshape(LK, 128, DK).transpose(1, 0, 2)

    return lay(cos), lay(sin)


def kernel(**inputs):
    import concourse.bacc as bacc
    from concourse.bass_utils import run_bass_kernel_spmd

    w = {n: np.asarray(a) for n, a in inputs.items()}
    f = np.float32
    ctx = w["ctx_512"]

    def columns(m):
        return m.T.reshape(KC, 128, -1).transpose(1, 0, 2).reshape(128, -1)

    def head_rows(parts):
        n = sum(p.shape[2] for p in parts)
        return np.concatenate(parts, 2).reshape(NP1, 2, 128, n).transpose(0, 2, 1, 3)

    cos, sin = rope_tables()
    up_down = np.stack([w["L0_ffn_W1"], w["L0_ffn_W2"]], 1)
    kc_q = w["L1_xattn_w_kc_q"].transpose(0, 2, 1).reshape(NH0, LK, 128, DK).transpose(0, 2, 1, 3)
    w_qr = w["L1_xattn_W_qr"].reshape(NH0, LK, 128, R1).transpose(0, 2, 1, 3)
    arrays = dict(
        x_in=w["x"],
        ctx_t_in=ctx.transpose(2, 0, 1),
        wq0_in=columns(w["L0_xattn_Wq"]),
        wkv0_in=w["L0_xattn_Wkv_expand"].T,
        wout0_in=columns(w["L0_xattn_Wout"]),
        ident_in=np.eye(128, dtype=f),
        mask_in=np.where(np.tril(np.ones((T, T), bool)), f(0), f(-1e30)).astype(f),
        wg_in=w["L0_ffn_Wg"].T.reshape(KC, 128, NE).transpose(1, 0, 2),
        w12_in=up_down.reshape(NE, 2, FH, KC, 128).transpose(0, 4, 1, 3, 2).reshape(NE, 128, W12),
        w3_in=w["L0_ffn_W3"].transpose(0, 2, 1),
        iota_in=np.tile(np.arange(NE, dtype=f), (T, 1)),
        ctxn_in=ctx,
        cos_in=cos,
        sin_in=sin,
        foldq_in=head_rows([kc_q.reshape(NH0, 128, LK * DK), w_qr.reshape(NH0, 128, LK * R1),
                            w["L1_xattn_Wq"].reshape(NH0, 128, D)]),
        krt_in=w["L1_xattn_W_kr"].transpose(0, 2, 1).reshape(NP1, 128, DK).transpose(1, 0, 2),
        foldp_in=head_rows([w["L1_xattn_w_kc_kv"], w["L1_xattn_Wo"].T.reshape(NH0, 128, D)]),
        wup_in=w["L1_ffn_w_gate_up"],
        wdown_in=w["L1_ffn_w_down"],
    )
    arrays = {n: np.ascontiguousarray(a) for n, a in arrays.items()}

    nc = bacc.Bacc("TRN2", target_bir_lowering=False, num_devices=1)
    args = [nc.dram_tensor(n, a.shape, mybir.dt.from_np(a.dtype), kind="ExternalInput").ap()
            for n, a in arrays.items()]
    args.append(nc.dram_tensor("out", (B, T, D), F32, kind="ExternalOutput").ap())
    build_kernel(nc, *args)
    r = run_bass_kernel_spmd(nc, [arrays], core_ids=[0])
    return r.results[0]["out"]
```

```python
import itertools
from contextlib import ExitStack

import numpy as np

import concourse.bass as bass
from concourse import mybir

F32 = mybir.dt.float32
F32R = mybir.dt.float32r
BF16 = mybir.dt.bfloat16
U32 = mybir.dt.uint32
ALU = mybir.AluOpType
ACT = mybir.ActivationFunctionType
AX = mybir.AxisListType

B, T, D = 8, 100, 512
KC = D // 128
LN_EPS = 1e-5
NH0, HD0, LAT = 16, 32, 128
HG = 128 // HD0
MT0 = NH0 // HG
NE, FH = 8, 352
FC = [128, 128, FH - 256]
HALF = B // 2 * T
W12, W3 = 2 * KC * FH, len(FC) * D
FI = 1408
IC = FI // 128
UT, DT = 2 * FI // 128, D // 128
GC = 4
GW_ = FI // GC
QMAX, QEPS = 127.0, 1e-8
MAGIC = 1.5 * 2 ** 23
NK, DK, LK, R1, CQ = 361, 128, 3, 64, 384
NP1 = NH0 // 2
ROWS = NH0 * T
RT = -(-ROWS // 128)
NG = -(-RT // 4)
LAG = 5
PVLAG = 2
ROPE_AT = [0, 1, 2, 4]
KVAT = LAG + 5
KBANK = 4 + (KVAT - LAG) % 3
NKE = NK + 1
FQ = LK * DK + LK * R1 + D
FP = DK + D


def layer_norm_steps(X, stats, mv, veps, std, rstd, s, ph):

    def batch(dve, n):
        dve.bn_stats(one(stats, n), one(X, n)).then_inc(s["stats"], 1)

    def vector(dve):
        dve.wait_ge(s["stats"], B * (ph + 1))
        for b in range(B):
            dve.bn_aggr(mv[:, b, :], stats[:, b, :]).then_inc(s["moments"], 1)
        dve.wait_ge(s["moments"], B * (ph + 1))
        dve.tensor_scalar(veps[:, :], mv[:, :, 1], LN_EPS, None, ALU.add).then_inc(s["var"], 1)
        dve.wait_ge(s["std"], ph + 1)
        dve.reciprocal(rstd[:, :], std[:, :]).then_inc(s["rstd"], 1)
        dve.wait_ge(s["rstd"], ph + 1)

    def scalar(act):
        act.wait_ge(s["var"], ph + 1)
        act.activation(std[:, :], veps[:, :], ACT.Sqrt).then_inc(s["std"], 1)

    return batch, vector, scalar


def one(t, n):
    return t[:, n, :] if isinstance(n, int) else t[:, bass.ds(n, 1), :].rearrange("p a d -> p (a d)")


def build_kernel(nc, x, ctx_t, wq0_t, wkv0_t, wout0_t, ident_d, mask_d, wg_t, w12_d, w3_d, iota_d,
                 ctxn_d, cos_d, sin_d, foldq_d, krt_d, foldp_d,
                 wup_d, wdown_d, out):
    with ExitStack() as top:
        def sem(name):
            return top.enter_context(nc.semaphore(name))

        def sems(phase, names):
            return {n: sem(f"{phase}_{n}") for n in names.split()}

        def sb_in(stack):
            return lambda name, shape, dt=F32: stack.enter_context(nc.sbuf_tensor(name, shape, dt))

        def ln_transposes(pe, ph, b):
            pe.wait_ge(LN["xn"], B * ph + b + 1)
            wait(pe, LN["lo"], B * ph + b - 1)
            for k in range(KC):
                last = pe.transpose(TP[b % 2][:, k, :], xn[:, b % 2, k * 128:(k + 1) * 128], ident[0:T, 0:T])
            last.then_inc(LN["xnt"], 1)

        def ln_high(act, ph, b, xh):
            act.wait_ge(LN["xnt"], B * ph + b + 1)
            act.copy(xh[:, :, b * T:(b + 1) * T], TP[b % 2]).then_inc(LN["hi"], 1)

        def ln_low(dve, ph, b, xh, xl):
            dve.wait_ge(LN["hi"], B * ph + b + 1)
            t = slice(b * T, (b + 1) * T)
            dve.tensor_tensor(xl[:, :, t], TP[b % 2], xh[:, :, t].bitcast(F32), ALU.subtract).then_inc(LN["lo"], 1)

        def normalise(dve, ph, b):
            wait(dve, LN["xnt"], B * ph + b - 1)
            dve.tensor_scalar(xn[:, b % 2, :], X[:, b, :], mv[:, b, 0:1], rstd[:, b:b + 1],
                              ALU.subtract, ALU.mult).then_inc(LN["xn"], 1)

        numbers = itertools.count()

        def wait(e, s, v):
            if isinstance(v, int):
                if v > 0:
                    e.wait_ge(s, v)
            elif v.min_val >= 0:
                e.wait_ge(s, v)
            else:
                count = e.alloc_register(f"count{next(numbers)}")
                e.reg_alu(count, v, 0, ALU.max)
                e.wait_ge(s, count)
                e.free_register(count)

        def mm3(pe, o, lh, ll, rh, rl, start, stop):
            pe.matmul(o, lh, rh, start=start, stop=False)
            pe.matmul(o, lh, rl, start=False, stop=False)
            return pe.matmul(o, ll, rh, start=False, stop=stop)

        sb = sb_in(top)
        X = sb("X", [T, B, D])
        ident = sb("ident", [128, 128])
        identb = sb("identb", [128, 128], BF16)
        stats = sb("stats", [T, B, 6])
        mv = sb("mv", [T, B, 2])
        veps = sb("veps", [T, B])
        std = sb("std", [T, B])
        rstd = sb("rstd", [T, B])
        xn = sb("xn", [T, 2, D])
        iota = sb("iota", [T, NE])
        wg = [sb("wg_raw", [128, KC, NE])] + [sb(f"wg_{n}", [128, KC, NE], F32R) for n in ("hi", "lo")]
        m_sb = [sb(f"m_sb{i}", [128, 2, R1]) for i in range(2)]
        wraw = sb("wraw", [128, W12 + W3])
        PS = top.enter_context(nc.psum_tensor("PS", [128, 8, 512], F32))

        pa = ExitStack()
        sa = sb_in(pa)
        NCX = B * T
        XH = sa("xnT_hi", [128, KC, NCX], F32R)
        XL = sa("xnT_lo", [128, KC, NCX], F32R)
        RAW_CTX, RAW_WKV, RAW_WQ, RAW_WO = 0, NCX, NCX + 2 * D, NCX + 2 * D + KC * D
        RAW_N = RAW_WO + KC * D
        raw0 = sa("raw0", [128, RAW_N])
        hi0 = sa("hi0", [128, RAW_N], F32R)
        lo0 = sa("lo0", [128, RAW_N], F32R)
        mask_f = sa("mask_f", [T, T])
        maskb = sa("maskb", [T, T], BF16)
        V = sa("V", [T, B, NH0, HD0 + 1])
        QT = sa("QT", [128, MT0, 2, T])
        KT = sa("KT", [128, MT0, 2, T])
        P0 = [sa(f"P0_{i}", [T, HG, MT0, T]) for i in range(2)]
        mx0 = sa("mx0", [T, 2, HG, MT0])
        PT = sa("PT0", [T, HG, MT0, T])
        rs0 = sa("rs0", [T, HG, MT0])
        O0 = sa("O0", [T, D])
        OH = sa("OH", [128, KC, T], F32R)
        OL = sa("OL", [128, KC, T], F32R)
        pa.close()

        pb = ExitStack()
        sbb = sb_in(pb)
        XHB = sbb("xnTb_hi", [128, KC, NCX], F32R)
        XLB = sbb("xnTb_lo", [128, KC, NCX], F32R)
        logits = sbb("logits", [T, B, NE])
        top8 = sbb("top8", [T, B, 8])
        top8i = sbb("top8i", [T, B, 8], U32)
        top2i = sbb("top2i", [T, B, 2])
        gd = sbb("gd", [T, 4, B])
        geq = sbb("geq", [T, 4, B, NE])
        GW = sbb("GW", [T, NE, B])
        wh = [sbb(f"we_hi{i}", [128, W12 + W3], F32R) for i in range(2)]
        wl = [sbb(f"we_lo{i}", [128, W12 + W3], F32R) for i in range(2)]
        silu = sbb("silu", [128, 2, HALF])
        h32 = sbb("h32", [128, 2, HALF])
        HH = sbb("hT_hi", [128, len(FC), NCX], F32R)
        HL = sbb("hT_lo", [128, len(FC), NCX], F32R)
        kr_raw = sbb("kr_raw", [128, NP1, DK])
        NFX = 5
        fq_more = [sbb(f"fq_raw{i}", [128, 2, FQ]) for i in range(NFX)]
        pb.close()

        pc = ExitStack()
        sc_ = sb_in(pc)
        XHC = sc_("xnTc_hi", [128, KC, NCX], F32R)
        XLC = sc_("xnTc_lo", [128, KC, NCX], F32R)
        NFH = sc_("nf_hi", [128, KC, NP1 * 128], F32R)
        NFL = sc_("nf_lo", [128, KC, NP1 * 128], F32R)
        WKH = sc_("wkr_hi", [128, NP1, DK], F32R)
        WKL = sc_("wkr_lo", [128, NP1, DK], F32R)
        QRH = sc_("qr_hi", [128, NP1, 2 * T], F32R)
        QRL = sc_("qr_lo", [128, NP1, 2 * T], F32R)
        QH = sc_("q_hi", [128, 2, ROWS], F32R)
        QL = sc_("q_lo", [128, 2, ROWS], F32R)
        cosr = sc_("cosr", [128, LK, DK])
        sinr = sc_("sinr", [128, LK, DK])
        kvraw = [sc_(f"kvraw{i}", [128, LK, DK]) for i in range(2)]
        kvt = [sc_(f"kvt{i}", [128, LK, DK]) for i in range(2)]
        kvr = sc_("kvr", [128, LK, DK])
        KNH = [sc_(f"kn_hi{i}", [128, LK, DK], F32R) for i in range(2)]
        KNL = [sc_(f"kn_lo{i}", [128, LK, DK], F32R) for i in range(2)]
        KTH = [sc_(f"kt_hi{i}", [128, NKE], F32R) for i in range(2)]
        KTL = [sc_(f"kt_lo{i}", [128, NKE], F32R) for i in range(2)]
        nmx = sc_("nmx", [128, 2, RT])
        rsum = sc_("rsum", [128, 2, RT])
        rinv = sc_("rinv", [128, 2, RT])
        ctxo = [sc_(f"ctxo{i}", [128, 512]) for i in range(2)]
        PTH = [sc_(f"pt_hi{i}", [128, LK, 512], F32R) for i in range(2)]
        PTL = [sc_(f"pt_lo{i}", [128, LK, 512], F32R) for i in range(2)]
        PTH.append(sc_("pt_hi_end", [128, LK, ROWS % 512], F32R))
        PTL.append(sc_("pt_lo_end", [128, LK, ROWS % 512], F32R))
        fp_more = [sc_(f"fp_raw{i}", [128, 2, FP]) for i in range(2)]
        pc.close()
        P1 = [wraw[:, i * 384:(i + 1) * 384] for i in range(8)]
        FQR = fq_more + [wraw[:, i * 2 * FQ:(i + 1) * 2 * FQ].rearrange("p (h n) -> p h n", h=2) for i in range(2)]
        FQR.append(fq_more[0])

        pd = ExitStack()
        sd = sb_in(pd)
        PFH = sd("pf_hi", [128, NH0, D], F32R)
        PFL = sd("pf_lo", [128, NH0, D], F32R)
        CXR = [sd(f"cx_raw{i}", [128, ROWS]) for i in range(2)]
        CXH = [sd(f"cx_hi{i}", [128, ROWS], F32R) for i in range(2)]
        CXL = [sd(f"cx_lo{i}", [128, ROWS], F32R) for i in range(2)]
        W1Q = sd("w1q", [128, KC, 2 * FI], BF16)
        W2Q = sd("w2q", [128, IC, D], BF16)
        S1B = sd("s1_rows", [T, 2 * FI])
        S2B = sd("s2_rows", [T, D])
        ones = sd("ones", [128, T])
        WQT = [sd(f"wq_tile{i}", [128, FI], BF16) for i in range(3)]
        wsc = [sd(f"wscale{i}", [128, 3]) for i in range(3)]
        diag = [sd(f"wdiag{i}", [128, 128]) for i in range(3)]
        mgc = sd("mgc", [128, 1])
        pd.close()
        WRT = [wraw[:, i * FI:(i + 1) * FI] for i in range(3)]
        pf_ = ExitStack()
        sf = sb_in(pf_)
        XM = [sf(f"xm{i}", [T, D]) for i in range(2)]
        XQ = [sf(f"xq{i}", [T, D], BF16) for i in range(2)]
        XQT = [sf(f"xqt{i}", [128, KC, T], BF16) for i in range(2)]
        sx = sf("sx", [T, 2, 3])
        sh = sf("sh", [T, 2, 4])
        hmx = sf("hmx", [T, 2, GC])
        GS = [sf(f"gs{i}", [T, GW_]) for i in range(2)]
        SL = [sf(f"sl{i}", [T, GW_]) for i in range(2)]
        US = [sf(f"us{i}", [T, GW_]) for i in range(2)]
        H1 = [sf(f"h1_{i}", [T, FI]) for i in range(2)]
        HQ = [sf(f"hq{i}", [T, FI], BF16) for i in range(2)]
        HQT = [sf(f"hqt{i}", [128, IC, T], BF16) for i in range(2)]
        Y2 = [sf(f"y2_{i}", [T, D]) for i in range(2)]
        pf_.close()
        FPR = fp_more + [wraw[:, i * 2 * FP:(i + 1) * 2 * FP].rearrange("p (h n) -> p h n", h=2) for i in range(2)]
        ctx_scratch = nc.dram_tensor("ctx_scratch", [B, 128, ROWS], F32, kind="Internal").ap()

        C = sems("c", "fq0 fq1 m msb nf nfh nfl kr krh krl cs kvz kv0 kv1 rot kvr "
                      "knh knl ktp kth ktl pr prh prl s max exp inv nrm pt pth ptl pv ctxo st0 st1")
        O = sems("o", "fp0 fp1 fp2 fp3 pf pfh pfl cx0 cx1 cxh cxl out res")

        LN = sems("ln", "stats moments var std rstd xn xnt hi lo")
        W = sems("w", "ld0 ld1 ld2 max sc inv mag sub tr ev dg bc sb ones mgc")
        F = sems("f", "xn xscale inv mag sub xt xev gps ups gs silu us h hmax hscale hinv hmag "
                      "hsub ht hev dn y res")

        A = sems("a", "x x2 consts wctx wwkv wwq wwo "
                      "cast whi wlo wlo2 vones vps vsb qk qsb ksb sc mx sub exp pt ptsb pv rs onorm ot oh ol op res")

        E = sems("e", "consts wghi wglo gate logits gating diff ex "
                      "d12 d3 hi12 lo12 hi3 lo3 gps ups silu hmul hhi hlo yps yacc zero")

        def part(t, at, *dims):
            n = int(np.prod(dims))
            v = t[:, at:at + n]
            if len(dims) == 2:
                return v.rearrange("p (a b) -> p a b", a=dims[0])
            return v

        wqh, wql = (part(t, RAW_WQ, KC, D) for t in (hi0, lo0))
        woh, wol = (part(t, RAW_WO, KC, D) for t in (hi0, lo0))
        wkvh, wkvl = (part(t, RAW_WKV, 2 * D) for t in (hi0, lo0))
        cxh, cxl = (part(t, RAW_CTX, B, T) for t in (hi0, lo0))
        SPLITS = [(RAW_CTX, RAW_WKV, "wctx"), (RAW_WKV, RAW_WQ, "wwkv"), (RAW_WQ, RAW_WO, "wwq"), (RAW_WO, RAW_N, "wwo")]
        S0 = [PS[0:T, i, 0:MT0 * T].rearrange("p (m k) -> p m k", m=MT0) for i in range(HG)]
        TP = [PS[:, 4, 0:KC * T].rearrange("p (m k) -> p m k", m=KC), PS[:, 5, 0:KC * T].rearrange("p (m k) -> p m k", m=KC)]
        OV = [PS[0:T, 6 + i, 0:2 * MT0 * (HD0 + 1)].rearrange("p (i m d) -> p i m d", i=2, m=MT0) for i in range(2)]
        INV0 = 1.0 / float(np.sqrt(np.float32(HD0)))
        ln_batch, ln_vec, ln_act = layer_norm_steps(X, stats, mv, veps, std, rstd, LN, 0)
        lnf_batch, lnf_vec, lnf_act = layer_norm_steps(X, stats, mv, veps, std, rstd, LN, 3)
        lnc_batch, lnc_vec, lnc_act = layer_norm_steps(X, stats, mv, veps, std, rstd, LN, 2)
        lne_batch, lne_vec, lne_act = layer_norm_steps(X, stats, mv, veps, std, rstd, LN, 1)

        def w12_of(t, which, k, c):
            at = (which * KC + k) * FH + c * 128
            return t[:, at:at + FC[c]]

        def w3_of(t, c):
            return t[0:FC[c], W12 + c * D:W12 + (c + 1) * D]

        def pair_steps(last, vector):
            ticks = [("S", b, t) for b in range(2) for t in range(RT)]
            ticks += [("PR", 2, k) for k in range(12)] if not last else []
            delay = {"PT": 1} if vector else {}
            due = []
            for b in range(2):
                for t in range(RT):
                    at = RT * b + t
                    at = at + LAG if at + LAG < 2 * RT else 2 * RT + 2 * (at + LAG - 2 * RT)
                    due.append((at, 1, ("PT", b, t)))
                    if t % 4 == 3:
                        due += [(at + PVLAG + c, 0, ("PV", b, t // 4 * LK + c)) for c in range(LK)]
                    elif t == RT - 1:
                        due += [(at + PVLAG + 2, 0, ("PV", b, t // 4 * LK + c)) for c in range(LK)]
                if b == 0 or not last:
                    due.append((RT * b + KVAT - 1, 2, ("KV", b + 1, 0)))
            placed = sorted((at + (delay.get(step[0], 0) if at + delay.get(step[0], 0) < 2 * RT else 0), at, order, step)
                            for at, order, step in due)
            out = []
            for i, tick in enumerate(ticks):
                out.append(tick)
                out += [step for at, _, _, step in placed if at == i]
            return out + [step for at, _, _, step in placed if at >= len(ticks)]

        def attention_steps(kind, vector=False):
            steps = pair_steps(kind == "last", vector)
            cut = steps.index(("S", 1, 0))
            steps = steps[:cut] if kind == "even" else [(w, b - 1, t) for w, b, t in steps[cut:]]
            return steps

        HTG = [(0, 6), (6, IC)]

        def earlier(t, ring):
            return t - ring if t >= ring else max(u for u in range(RT) if u % ring == t) - RT

        def tile_rows(t):
            return min(128, ROWS - 128 * t)

        def wtiles(n, odd):
            if isinstance(n, int) and n == B:
                return [("up", UT - 2), ("up", UT - 1)]
            p = (n[0] if isinstance(n, tuple) else n // 2)
            return [("up", 5 * p + 3), ("up", 5 * p + 4), ("down", p)] if odd else [("up", 5 * p + i) for i in range(3)]

        def cols_at(i, width):
            return slice(i * width, (i + 1) * width) if isinstance(i, int) else bass.ds(i * width, width)

        def wbank(i, chunks):
            b = PS[:, i, :] if i < 2 else PS[:, 2:4, :].rearrange("p a n -> p (a n)")
            return b.bitcast(BF16)[:, 0:chunks * 128].rearrange("p (c n) -> p c n", c=chunks)

        OUTS = [sem("out_stored0"), sem("out_stored1")]
        block = top.enter_context(nc.Block())

        @block.sync
        def _(sp):
            xr = x.rearrange("b t d -> t b d")
            sp.dma_start(X[:, 0:B // 2, :], xr[:, 0:B // 2, :]).then_inc(A["x"], 16)
            sp.dma_start(X[:, B // 2:B, :], xr[:, B // 2:B, :]).then_inc(A["x2"], 16)
            sp.dma_start(ident[:, :], ident_d).then_inc(A["consts"], 16)
            sp.dma_start(mask_f[:, :], mask_d).then_inc(A["consts"], 16)
            sp.dma_start(part(raw0, RAW_CTX, B, T), ctx_t[:, :, 0:T]).then_inc(A["wctx"], 16)
            sp.dma_start(part(raw0, RAW_WKV, 2 * D), wkv0_t).then_inc(A["wwkv"], 16)
            sp.dma_start(part(raw0, RAW_WQ, KC * D), wq0_t).then_inc(A["wwq"], 16)
            sp.dma_start(part(raw0, RAW_WO, KC * D), wout0_t).then_inc(A["wwo"], 16)
            sp.dma_start(iota[:, :], iota_d).then_inc(E["consts"], 16)
            sp.dma_start(wg[0][:, :, :], wg_t).then_inc(E["consts"], 16)

            def load_expert(e):
                w12s = w12_d[e] if isinstance(e, int) else w12_d[bass.ds(e, 1)].rearrange("o p n -> (o p) n")
                w3s = w3_d[e] if isinstance(e, int) else w3_d[bass.ds(e, 1)].rearrange("o h n -> (o h) n")
                wait(sp, E["lo12"], e)
                sp.dma_start(wraw[:, 0:W12], w12s).then_inc(E["d12"], 16)
                wait(sp, E["lo3"], e)
                whole = len(FC) - 1
                if isinstance(e, int) and e == 0:
                    sp.wait_ge(E["zero"], 1)
                sp.dma_start(wraw[:, W12:W12 + whole * D].rearrange("p (c n) -> p c n", c=whole),
                             w3s[0:whole * 128].rearrange("(c p) n -> p c n", p=128)).then_inc(E["d3"], 16)
                sp.dma_start(wraw[0:FC[-1], W12 + whole * D:W12 + W3], w3s[whole * 128:FH]).then_inc(E["d3"], 16)

            load_expert(0)
            load_expert(1)
            sp.wait_ge(A["res"], B)
            sp.dma_start(kr_raw[:, :, :], krt_d).then_inc(C["kr"], 16)
            for i in range(NFX):
                sp.dma_start(FQR[i][:, :, :], foldq_d[i]).then_inc(C["fq0"], 16)
            with sp.Fori(2, NE) as e:
                load_expert(e)
            sp.wait_ge(E["lo12"], NE)
            sp.wait_ge(E["lo3"], NE)
            for i in range(NFX, NP1 - 1):
                sp.dma_start(FQR[i], foldq_d[i]).then_inc(C["fq1"], 16)
            sp.wait_ge(E["yacc"], B * NE)
            sp.dma_start(cosr[:, :, :], cos_d).then_inc(C["cs"], 16)
            sp.dma_start(sinr[:, :, :], sin_d).then_inc(C["cs"], 16)

            def load_kv(n, j):
                if isinstance(n, int) and n < 2:
                    sp.wait_ge(C["kvz"], 2)
                wait(sp, C["rot"], 3 * (n - 1))
                kvn = ctxn_d[n] if isinstance(n, int) else ctxn_d[bass.ds(n, 1)].rearrange("o l d -> (o l) d")
                whole = LK - 1
                sp.dma_start(kvraw[j][:, 0:whole, :], kvn[0:whole * 128].rearrange("(c p) d -> p c d", p=128)) \
                    .then_inc(C[f"kv{j}"], 16)
                sp.dma_start(kvraw[j][0:NK - whole * 128, whole, :], kvn[whole * 128:NK]).then_inc(C[f"kv{j}"], 16)

            load_kv(0, 0)
            load_kv(1, 1)
            sp.wait_ge(C["nf"], 1)
            sp.dma_start(FQR[NP1 - 1][:, :, :], foldq_d[NP1 - 1]).then_inc(C["fq0"], 16)

            def load_foldp(i):
                if 2 <= i < 4:
                    wait(sp, C["pt"], RT * B)
                wait(sp, O["pf"], 2 * (i - 3))
                sp.dma_start(FPR[i % 4][:, :, :], foldp_d[i]).then_inc(O[f"fp{i % 4}"], 16)

            sp.wait_ge(C["nf"], NP1)
            load_foldp(0)
            load_foldp(1)

            def store_ctx(n, g):
                cols = min(512, ROWS - g * 512)
                wait(sp, C["ctxo"], NG * n + g + 1)
                dst = ctx_scratch[n] if isinstance(n, int) else ctx_scratch[bass.ds(n, 1)].rearrange("o p r -> (o p) r")
                sp.dma_start(dst[:, g * 512:g * 512 + cols], ctxo[g % 2][:, 0:cols]).then_inc(C[f"st{g % 2}"], 16)

            def store_batch(n, j, more=True):
                if more:
                    load_kv(n + 2, j)
                for g in range(NG):
                    store_ctx(n, g)

            with sp.Fori(0, B // 2 - 1) as p:
                store_batch(2 * p, 0)
                store_batch(2 * p + 1, 1)
            store_batch(B - 2, 0, False)
            store_batch(B - 1, 1, False)

            def load_ctx(n, j):
                if isinstance(n, int) and n == 0:
                    sp.wait_ge(C["st0"], 16 * NG // 2 * B)
                    sp.wait_ge(C["st1"], 16 * NG // 2 * B)
                wait(sp, O["cxl"], n - 1)
                src = ctx_scratch[n] if isinstance(n, int) else ctx_scratch[bass.ds(n, 1)].rearrange("o p r -> (o p) r")
                sp.dma_start(CXR[j][:, :], src).then_inc(O[f"cx{j}"], 16)

            load_foldp(2)
            load_foldp(3)
            load_ctx(0, 0)
            load_ctx(1, 1)
            for i in range(4, NP1):
                load_foldp(i)
            with sp.Fori(1, B // 2) as p:
                load_ctx(2 * p, 0)
                load_ctx(2 * p + 1, 1)
            def store_out(n, j):
                wait(sp, F["res"], n + 1)
                o = out[n] if isinstance(n, int) else out[bass.ds(n, 1)].rearrange("o t d -> (o t) d")
                xs = X[:, n, :] if isinstance(n, int) else X[:, bass.ds(n, 1), :].rearrange("p a d -> p (a d)")
                sp.dma_start(o, xs).then_inc(OUTS[j], 16)

            with sp.Fori(0, B // 2) as p:
                store_out(2 * p, 0)
                store_out(2 * p + 1, 1)
            sp.wait_ge(OUTS[0], 16 * B // 2)
            sp.wait_ge(OUTS[1], 16 * B // 2)

        @block.gpsimd
        def _(pool):
            pool.wait_ge(A["consts"], 32)
            pool.tensor_copy(identb[:, :], ident[:, :]).then_inc(A["cast"], 1)
            pool.tensor_copy(maskb[:, :], mask_f[:, :]).then_inc(A["cast"], 1)
            pool.memset(V[:, :, :, :], 1.0).then_inc(A["vones"], 1)
            pool.wait_ge(A["vones"], 1)
            pool.memset(wraw[FC[-1]:128, W12 + (len(FC) - 1) * D:W12 + W3], 0.0).then_inc(E["zero"], 1)
            pool.wait_ge(E["zero"], 1)

            for k in (2, 3):
                a, z, _ = SPLITS[k]
                pool.wait_ge(A["whi"], k + 1)
                pool.tensor_tensor(lo0[:, a:z], raw0[:, a:z], hi0[:, a:z].bitcast(F32), ALU.subtract).then_inc(A["wlo2"], 1)

            def split_low(e, j):
                wait(pool, E["hi12"], e + 1)
                pool.tensor_tensor(wl[j][:, 0:W12], wraw[:, 0:W12], wh[j][:, 0:W12].bitcast(F32), ALU.subtract) \
                    .then_inc(E["lo12"], 1)
                wait(pool, E["hi3"], e + 1)
                pool.tensor_tensor(wl[j][:, W12:], wraw[:, W12:], wh[j][:, W12:].bitcast(F32), ALU.subtract) \
                    .then_inc(E["lo3"], 1)

            with pool.Fori(0, NE // 2) as i:
                split_low(2 * i, 0)
                split_low(2 * i + 1, 1)

            pool.wait_ge(E["yacc"], B * NE)
            tail = (NK - 256) // 32 * 32
            for j in range(2):
                pool.memset(kvraw[j][tail:128, LK - 1, :], 0.0).then_inc(C["kvz"], 1)
                pool.wait_ge(C["kvz"], j + 1)

            def rope(n, j, part):
                h = DK // 2
                if part == 0:
                    wait(pool, C[f"kv{j}"], 16 * n + 32 - 16 * j)
                    if isinstance(n, int) and n == 0:
                        pool.wait_ge(C["cs"], 32)
                    wait(pool, C["kvr"], n)
                    pool.tensor_tensor(kvt[0][:, :, :], kvraw[j][:, :, :], cosr[:, :, :], ALU.mult).then_inc(C["rot"], 1)
                elif part == 1:
                    pool.tensor_tensor(kvt[1][:, :, 0:h], kvraw[j][:, :, h:DK], sinr[:, :, 0:h], ALU.mult).then_inc(C["rot"], 1)
                elif part == 2:
                    pool.tensor_tensor(kvt[1][:, :, h:DK], kvraw[j][:, :, 0:h], sinr[:, :, h:DK], ALU.mult).then_inc(C["rot"], 1)
                else:
                    wait(pool, C["rot"], 3 * n + 3)
                    wait(pool, C["ktp"], n)
                    wait(pool, C["knl"], n)
                    pool.tensor_tensor(kvr[:, :, :], kvt[0][:, :, :], kvt[1][:, :, :], ALU.add).then_inc(C["kvr"], 1)

            def rope_low(n, j):
                wait(pool, C["knh"], n + 1)
                pool.tensor_tensor(KNL[j][:, :, :], kvr[:, :, :], KNH[j][:, :, :].bitcast(F32), ALU.subtract).then_inc(C["knl"], 1)

            def pool_steps(kind, n, j):
                for step in attention_steps(kind):
                    what, dn, t = step
                    m, jj = (n, j) if dn == 0 else (n + dn, 1 - j)
                    if what == "S":
                        rows = min(128, ROWS - 128 * t)
                        slot = t % 8
                        wait(pool, C["inv"], RT * m + t + 1)
                        pool.tensor_tensor(P1[slot][0:rows, 0:NK], P1[slot][0:rows, 0:NK],
                                           rinv[0:rows, jj, t:t + 1].broadcast_to((rows, NK)), ALU.mult).then_inc(C["nrm"], 1)
                        if kind != "last" and t in ROPE_AT:
                            rope(n + 1, 1 - j, ROPE_AT.index(t))
                    elif what == "KV":
                        rope_low(n + 1, 1 - j)

            wait(pool, C["nf"], NP1)
            for slot in range(8):
                pool.memset(P1[slot][:, NK:384], 0.0).then_inc(C["kvz"], 1)
            pool.wait_ge(C["kvz"], 10)
            for part in range(4):
                rope(0, 0, part)
            rope_low(0, 0)
            pool_steps("even", 0, 0)
            with pool.Fori(0, B // 2 - 1) as p:
                pool_steps("odd", 2 * p + 1, 1)
                pool_steps("even", 2 * p + 2, 0)
            pool_steps("last", B - 1, 1)

            def load_tile(n, i, kind, at):
                wait(pool, W["sub"], 3 * (n - 1) + i + 1)
                if kind == "up":
                    src, dst = wup_d, WRT[i][:, 0:D]
                else:
                    src, dst = wdown_d, WRT[i]
                pool.dma_start(dst, src[cols_at(at, 128), :]).then_inc(W[f"ld{i}"], 16)

            def diagonal(n, i):
                wait(pool, W["sc"], 3 * n + i + 1)
                wait(pool, W["bc"], 3 * (n - 1) + i + 1)
                pool.tensor_tensor(diag[i][:, :], ident[:, :], wsc[i][:, 1:2].broadcast_to((128, 128)), ALU.mult) \
                    .then_inc(W["dg"], 1)

            def pool_weights(n, odd, p=None, more=None):
                for i, _ in enumerate(wtiles(n if p is None else (p,), odd)):
                    diagonal(n, i)
                if more is not None:
                    for i, (kind, at) in enumerate(more):
                        load_tile(n + 1, i, kind, at)

            pool.wait_ge(O["pf"], NH0)
            pool.memset(ones[:, :], 1.0).then_inc(W["ones"], 1)
            pool.wait_ge(W["ones"], 1)
            pool.memset(mgc[:, :], MAGIC).then_inc(W["mgc"], 1)
            pool.wait_ge(W["mgc"], 1)
            for i, (kind, at) in enumerate(wtiles(0, False)):
                load_tile(0, i, kind, at)
            with pool.Fori(0, B // 2 - 1) as p:
                pool_weights(2 * p, False, p, wtiles((p,), True))
                pool_weights(2 * p + 1, True, p, wtiles((p + 1,), False))
            pool_weights(B - 2, False, None, wtiles(B - 1, True))
            pool_weights(B - 1, True, None, wtiles(B, False))
            pool_weights(B, False)

            def pool_h(m, j):
                for c in range(GC):
                    wait(pool, F["us"], GC * m + c + 1)
                    wait(pool, F["silu"], GC * m + c + 1)
                    if c == 0:
                        wait(pool, F["hsub"], m - 1)
                    pool.tensor_tensor(H1[j][:, c * GW_:(c + 1) * GW_], SL[c % 2][:, :], US[c % 2][:, :], ALU.mult) \
                        .then_inc(F["h"], 1)

            def pool_add(n, j):
                wait(pool, F["y"], n + 1)
                xs = X[:, n, :] if isinstance(n, int) else X[:, bass.ds(n, 1), :].rearrange("p a d -> p (a d)")
                pool.tensor_tensor(xs, xs, Y2[j][:, :], ALU.add).then_inc(F["res"], 1)

            pool_h(0, 0)
            with pool.Fori(0, B // 2 - 1) as p:
                pool_h(2 * p + 1, 1)
                pool_add(2 * p, 0)
                pool_h(2 * p + 2, 0)
                pool_add(2 * p + 1, 1)
            pool_h(B - 1, 1)
            pool_add(B - 2, 0)
            pool_add(B - 1, 1)

        NCH = len(FC)

        def act_gu(act, e, half):
            for c in range(NCH):
                step, par = NCH * (2 * e + half) + c, (half + c) % 2
                r = slice(0, FC[c])
                wait(act, E["gps"], step + 1)
                wait(act, E["hmul"], step - 1)
                act.activation(silu[r, par, :], PS[r, par, 0:HALF], ACT.Silu).then_inc(E["silu"], 1)
            for c in range(NCH):
                step, par = NCH * (2 * e + half) + c, (half + c) % 2
                r = slice(0, FC[c])
                wait(act, E["hmul"], step + 1)
                if c == 0:
                    wait(act, E["yps"], 4 * (2 * e + half - 1))
                act.copy(HH[r, c, half * HALF:(half + 1) * HALF], h32[r, par, :]).then_inc(E["hhi"], 1)

        def act_attn0_exp(act, n, j):
            for i in range(HG):
                wait(act, A["sub"], HG * n + i + 1)
                act.activation(P0[j][:, i, :, :], P0[j][:, i, :, :], ACT.Exp, scale=INV0).then_inc(A["exp"], 1)

        def act_attn0_q(act, p):
            for m in range(MT0):
                wait(act, A["qk"], 2 * MT0 * p + 2 * m + 1)
                if m == 0:
                    wait(act, A["sc"], 2 * HG * p)
                act.copy(QT[:, m, :, :], PS[:, 6, 0:2 * T].rearrange("p (b t) -> p b t", b=2)).then_inc(A["qsb"], 1)

        def act_attn0_pt(act, n):
            for i in range(HG):
                wait(act, A["pt"], (HG + 0) * n + i + 1)
                if i == 0:
                    wait(act, A["pv"], 2 * n)
                act.copy(PT[:, i, :, :], TP[i % 2][0:T]).then_inc(A["ptsb"], 1)

        def act_attn0_oh(act, n):
            wait(act, A["ot"], n + 1)
            wait(act, A["op"], n)
            act.copy(OH[:, :, :], TP[0]).then_inc(A["oh"], 1)

        def act_fold_m(act, i, j):
            wait(act, C["m"], i + 1)
            wait(act, C["nf"], i - 1)
            act.copy(m_sb[j][:, :, :], PS[:, j, 0:2 * R1].rearrange("p (h r) -> p h r", h=2)).then_inc(C["msb"], 1)

        def fold_cols(t, i):
            return t[:, :, i * 128:(i + 1) * 128] if isinstance(i, int) else t[:, :, bass.ds(i * 128, 128)]

        def act_fold_n(act, i, j):
            wait(act, C["nf"], i + 1)
            act.copy(fold_cols(NFH, i), PS[:, 2 + j, :].rearrange("p (k n) -> p k n", k=KC)).then_inc(C["nfh"], 1)

        def queries_part(k, hi):
            if k < 4:
                o = (QRH if hi else QRL)[:, 2 * k:2 * k + 2, :]
                return o, PS[:, k % 4, 0:4 * T].rearrange("p (m t) -> p m t", m=2)
            h0 = (k - 4) // 2 * 4 + k % 2
            o = (QH if hi else QL)[:, :, :].rearrange("p j (h t) -> p h j t", t=T)[:, h0:h0 + 3:2]
            return o, PS[:, k % 4, 0:4 * T].rearrange("p (h j t) -> p h j t", h=2, j=2)

        def act_queries(act, q, k):
            wait(act, C["pr"], 12 * q + k + 1)
            o, bank = queries_part(k, True)
            act.copy(o, bank).then_inc(C["prh"], 1)

        def turned(t):
            return PS[:, 4 + t % 3, 0:LK * 128].rearrange("p (c r) -> p c r", c=LK)[:, :, 0:tile_rows(t)]

        def pt_buffer(g, j):
            return 2 if g == NG - 1 else (g + j * (NG - 1)) % 2

        def pt_free(m, g):
            return NG * m if g == NG - 1 else NG * m + g - 1 if g >= 2 else NG * (m - 1) + g + 2

        def pt_place(buf, t, j):
            return buf[pt_buffer(t // 4, j)][:, :, t % 4 * 128:t % 4 * 128 + tile_rows(t)]

        def act_keys(act, n, j):
            wait(act, C["ktp"], n + 1)
            act.copy(KTH[j][:, :], PS[:, KBANK, 0:NKE]).then_inc(C["kth"], 1)
            wait(act, C["pv"], NG * (n - 1))
            wait(act, C["kvr"], n + 1)
            act.copy(KNH[j][:, :, :], kvr[:, :, :]).then_inc(C["knh"], 1)

        def act_steps(act, kind, n, j, q=None):
            for what, dn, t in attention_steps(kind):
                m, jj = (n, j) if dn == 0 else (n + dn, 1 - j)
                if what == "S":
                    r = slice(0, tile_rows(t))
                    wait(act, C["max"], RT * m + t + 1)
                    wait(act, C["pt"], RT * m + earlier(t, 8) + 1)
                    act.activation(P1[t % 8][r, 0:NK], PS[r, t % 4, 0:NK], ACT.Exp, bias=nmx[r, jj, t:t + 1],
                                   accum_out=rsum[r, jj, t:t + 1]).then_inc(C["exp"], 1)
                elif what == "PT":
                    wait(act, C["pt"], RT * m + t + 1)
                    if t % 4 == 0:
                        wait(act, C["pv"], pt_free(m, t // 4))
                    act.copy(pt_place(PTH, t, jj), turned(t)).then_inc(C["pth"], 1)
                elif what == "PV":
                    t, c = divmod(t, LK)
                    if c < LK - 1:
                        continue
                    cols = min(512, ROWS - t * 512)
                    wait(act, C["pv"], NG * m + t + 1)
                    wait(act, C[f"st{t % 2}"], 16 * (NG // 2) * m + 16 * (t // 2))
                    act.copy(ctxo[t % 2][:, 0:cols], PS[:, 7, 0:cols]).then_inc(C["ctxo"], 1)
                elif what == "KV":
                    act_keys(act, n + 1, 1 - j)
                elif what == "PR":
                    act_queries(act, q, t)

        @block.scalar
        def _(act):
            for k, (a, z, name) in enumerate(SPLITS[:2]):
                act.wait_ge(A[name], 16)
                act.copy(hi0[:, a:z], raw0[:, a:z]).then_inc(A["whi"], 1)
            ln_act(act)
            for b in range(B + 2):
                if b < B:
                    ln_high(act, 0, b, XH)
                if b in (1, 3):
                    a, z, name = SPLITS[2 + b // 2]
                    act.wait_ge(A[name], 16)
                    act.copy(hi0[:, a:z], raw0[:, a:z]).then_inc(A["whi"], 1)
                if b < 2:
                    continue
                if b == 2:
                    act.wait_ge(A["vones"], 1)
                v = b - 2
                act.wait_ge(A["vps"], v + 1)
                act.copy(V[:, v, :, 0:HD0], PS[0:T, v % 2, :].rearrange("p (h d) -> p h d", h=NH0)).then_inc(A["vsb"], 1)
            def batch(n, j, queries=None):
                act_attn0_pt(act, n)
                if not (isinstance(n, int) and n == 0):
                    act_attn0_oh(act, n - 1)
                if queries is not None:
                    act_attn0_q(act, queries)
                if not (isinstance(n, int) and n == B - 1):
                    act_attn0_exp(act, n + 1, 1 - j)

            act_attn0_q(act, 0)
            act_attn0_exp(act, 0, 0)
            batch(0, 0, 1)
            with act.Fori(0, B // 2 - 2) as p:
                batch(2 * p + 1, 1)
                batch(2 * p + 2, 0, p + 2)
            for n in range(B - 3, B):
                batch(n, n % 2)
            act_attn0_oh(act, B - 1)
            lne_act(act)
            act.wait_ge(E["consts"], 32)
            act.copy(wg[1][:, :, :], wg[0][:, :, :]).then_inc(E["wghi"], 1)
            for b in range(B):
                ln_high(act, 1, b, XHB)
            act.wait_ge(E["diff"], 1)
            act.activation(gd[:, 1, :], gd[:, 0, :], ACT.Exp).then_inc(E["ex"], 1)
            act_gu(act, 0, 0)
            with act.Fori(0, NE // 2 - 1) as i:
                act_gu(act, 2 * i, 1)
                act_gu(act, 2 * i + 1, 0)
                act_gu(act, 2 * i + 1, 1)
                act_gu(act, 2 * i + 2, 0)
            act_gu(act, NE - 2, 1)
            act_gu(act, NE - 1, 0)
            act_gu(act, NE - 1, 1)
            act_fold_m(act, 0, 0)
            lnc_act(act)
            act.wait_ge(C["kr"], 16)
            act.copy(WKH[:, :, :], kr_raw[:, :, :]).then_inc(C["krh"], 1)
            for i in range(NP1):
                if i + 1 < NP1:
                    act_fold_m(act, i + 1, (i + 1) % 2)
                act_fold_n(act, i, i % 2)
            for b in range(B):
                ln_high(act, 2, b, XHC)
            act_keys(act, 0, 0)
            for k in range(12):
                act_queries(act, 0, k)
            act_steps(act, "even", 0, 0)
            with act.Fori(0, B // 2 - 1) as p:
                act_steps(act, "odd", 2 * p + 1, 1, p + 1)
                act_steps(act, "even", 2 * p + 2, 0)
            act_steps(act, "last", B - 1, 1)
            def split_ctx(n, j):
                wait(act, O[f"cx{j}"], 8 * n + 16 - 8 * j)
                wait(act, O["out"], n - 1)
                act.copy(CXH[j][:, :], CXR[j][:, :]).then_inc(O["cxh"], 1)

            for h in range(NH0):
                act.wait_ge(O["pf"], h + 1)
                act.copy(PFH[:, h, :], PS[:, h % 4, :]).then_inc(O["pfh"], 1)
                if h == NH0 - 4:
                    split_ctx(0, 0)

            def act_weights(n, odd, p=None):
                tiles = wtiles(n if p is None else (p,), odd)
                for i, (kind, _) in enumerate(tiles):
                    wait(act, W["inv"], 3 * n + i + 1)
                    raw = WRT[i][:, 0:D] if kind == "up" else WRT[i]
                    act.activation(raw, raw, ACT.Identity, bias=mgc[:, 0:1], scale=wsc[i][:, 2:3]).then_inc(W["mag"], 1)
                for i, (kind, at) in enumerate(tiles):
                    wait(act, W["tr"], 3 * n + i + 1)
                    o, ch = (W1Q, KC) if kind == "up" else (W2Q, IC)
                    act.copy(o[:, :, cols_at(at, 128)], wbank(i, ch)).then_inc(W["ev"], 1)

            act.wait_ge(W["mgc"], 1)
            with act.Fori(0, B // 2 - 1) as p:
                split_ctx(2 * p + 1, 1)
                act_weights(2 * p, False, p)
                split_ctx(2 * p + 2, 0)
                act_weights(2 * p + 1, True, p)
            split_ctx(B - 1, 1)
            act_weights(B - 2, False)
            act_weights(B - 1, True)
            lnf_act(act)
            act_weights(B, False)


            def act_xq(m, j):
                wait(act, F["inv"], m + 1)
                wait(act, F["sub"], m - 1)
                act.activation(XM[j][:, :], xn[:, j, :], ACT.Identity, bias=mgc[0:T, 0:1], scale=sx[:, j, 2:3]) \
                    .then_inc(F["mag"], 1)

            def act_xev(m, j):
                wait(act, F["xt"], m + 1)
                wait(act, F["ups"], GC * (m - 1))
                act.copy(XQT[j][:, :, :], PS[:, 6, :].bitcast(BF16)[:, 0:KC * T].rearrange("p (k t) -> p k t", k=KC)) \
                    .then_inc(F["xev"], 1)

            def act_silu(m, c):
                wait(act, F["gs"], GC * m + c + 1)
                wait(act, F["h"], GC * m + c - 1)
                act.activation(SL[c % 2][:, :], GS[c % 2][:, :], ACT.Silu).then_inc(F["silu"], 1)

            def act_hq(n, j):
                wait(act, F["hinv"], n + 1)
                act.activation(H1[j][:, :], H1[j][:, :], ACT.Identity, bias=mgc[0:T, 0:1], scale=sh[:, j, 2:3]) \
                    .then_inc(F["hmag"], 1)

            def act_hev(n, j):
                for g, (a, z) in enumerate(HTG):
                    wait(act, F["ht"], 2 * n + g + 1)
                    act.copy(HQT[j][:, a:z, :], PS[:, 4 + g, :].bitcast(BF16)[:, 0:(z - a) * T]
                             .rearrange("p (k t) -> p k t", k=z - a)).then_inc(F["hev"], 1)

            def act_ffn(n, j, more=True):
                act_silu(n + 1, 0)
                act_hq(n, j)
                act_silu(n + 1, 1)
                if more:
                    act_xq(n + 2, j)
                act_silu(n + 1, 2)
                act_hev(n, j)
                act_silu(n + 1, 3)
                if more:
                    act_xev(n + 2, j)

            act_xq(0, 0)
            act_xev(0, 0)
            act_xq(1, 1)
            for c in range(GC):
                act_silu(0, c)
                if c == 1:
                    act_xev(1, 1)
            with act.Fori(0, B // 2 - 1) as p:
                act_ffn(2 * p, 0)
                act_ffn(2 * p + 1, 1)
            act_ffn(B - 2, 0, False)
            act_hq(B - 1, 1)
            act_hev(B - 1, 1)

        def pe_gu(pe, e, half, j):
            t = slice(half * HALF, (half + 1) * HALF)
            wait(pe, E["lo12"], e + 1)
            for c in range(NCH):
                step, par = NCH * (2 * e + half) + c, (half + c) % 2
                for which, free, done in ((0, "silu", "gps"), (1, "hmul", "ups")):
                    wait(pe, E[free], step - 1)
                    for k in range(KC):
                        last = mm3(pe, PS[0:FC[c], 2 * which + par, 0:HALF], w12_of(wh[j], which, k, c),
                                   w12_of(wl[j], which, k, c), XHB[:, k, t], XLB[:, k, t], k == 0, k == KC - 1)
                    last.then_inc(E[done], 1)

        def pe_y(pe, e, half, j):
            u = 2 * e + half
            wait(pe, E["lo3"], e + 1)
            wait(pe, E["hlo"], NCH * (u + 1))
            for q in range(B // 2):
                wait(pe, E["yacc"], B // 2 * (u - 1) + q + 1)
                t = slice((half * 4 + q) * T, (half * 4 + q + 1) * T)
                for c in range(NCH):
                    r = slice(0, FC[c])
                    last = mm3(pe, PS[0:T, 4 + q, :], HH[r, c, t], HL[r, c, t], w3_of(wh[j], c), w3_of(wl[j], c),
                               c == 0, c == NCH - 1)
                last.then_inc(E["yps"], 1)

        def pe_attn0_qk(pe, p):
            if isinstance(p, int):
                xh, xl = XH[:, :, p * 2 * T:(p + 1) * 2 * T], XL[:, :, p * 2 * T:(p + 1) * 2 * T]
            else:
                xh, xl = XH[:, :, bass.ds(p * (2 * T), 2 * T)], XL[:, :, bass.ds(p * (2 * T), 2 * T)]
            for m in range(MT0):
                wait(pe, A["qsb"], MT0 * p + m)
                if m == 0:
                    wait(pe, A["onorm"], 4 * p - 4)
                for k in range(KC):
                    last = mm3(pe, PS[:, 6, 0:2 * T], wqh[:, k, m * 128:(m + 1) * 128], wql[:, k, m * 128:(m + 1) * 128],
                               xh[:, k], xl[:, k], k == 0, k == KC - 1)
                last.then_inc(A["qk"], 1)
                wait(pe, A["ksb"], MT0 * p + m)
                if isinstance(p, int):
                    ch, cl = cxh[:, 2 * p:2 * p + 2, :], cxl[:, 2 * p:2 * p + 2, :]
                else:
                    ch, cl = cxh[:, bass.ds(p * 2, 2), :], cxl[:, bass.ds(p * 2, 2), :]
                mm3(pe, PS[:, 7, 0:2 * T], wkvh[:, m * 128:(m + 1) * 128], wkvl[:, m * 128:(m + 1) * 128],
                    ch.rearrange("p b t -> p (b t)"), cl.rearrange("p b t -> p (b t)"), True, True).then_inc(A["qk"], 1)

        def pe_attn0_scores(pe, n, j):
            for i in range(HG):
                wait(pe, A["sub"], HG * (n - 1) + i + 1)
                pe.matmul(S0[i], identb[0:T, 0:T], maskb[:, None, :].broadcast_to((T, MT0, T)), start=True, stop=False)
            wait(pe, A["qsb"], 2 * n + 4 - 2 * j)
            wait(pe, A["ksb"], 2 * n + 4 - 2 * j)
            for m in range(MT0):
                for i in range(HG):
                    r = slice(i * HD0, (i + 1) * HD0)
                    last = pe.matmul(S0[i][:, m, :], QT[r, m, j, :], KT[r, m, j, :], start=False, stop=(m == MT0 - 1),
                                     tile_position=(i * HD0, 0))
                    if m == MT0 - 1:
                        last.then_inc(A["sc"], 1)

        def pe_attn0_pt(pe, n, j):
            for i in range(HG):
                wait(pe, A["exp"], HG * n + i + 1)
                if i == 0:
                    wait(pe, A["ol"], n - 1)
                elif i == 1:
                    wait(pe, A["res"], n - 1)
                else:
                    wait(pe, A["ptsb"], HG * n + i - 1)
                for m in range(MT0):
                    last = pe.transpose(TP[i % 2][0:T, m, :], P0[j][:, i, m, :], ident[0:T, 0:T])
                last.then_inc(A["pt"], 1)

        def pe_attn0_pv(pe, n, j):
            if j == 0 and not (isinstance(n, int) and n == B - 2):
                wait(pe, A["qsb"], 2 * n + 2 * MT0)
                wait(pe, A["ksb"], 2 * n + 2 * MT0)
            for g in range(2):
                wait(pe, A["onorm"], 2 * (n - 1) + g + 1)
                for i in (2 * g, 2 * g + 1):
                    wait(pe, A["ptsb"], HG * n + i + 1)
                    for m in range(MT0):
                        v = V[:, n, m * HG + i, :] if isinstance(n, int) else \
                            V[:, bass.ds(n, 1), m * HG + i, :].rearrange("p a d -> p (a d)")
                        last = pe.matmul(OV[g][:, i % 2, m, :], PT[:, i, m, :], v, start=True, stop=True)
                last.then_inc(A["pv"], 1)

        def pe_attn0_ot(pe, n):
            wait(pe, A["onorm"], 2 * n + 2)
            if not (isinstance(n, int) and n == B - 1):
                wait(pe, A["ptsb"], HG * (n + 1) + 3)
            for k in range(KC):
                last = pe.transpose(TP[0][:, k, :], O0[:, k * 128:(k + 1) * 128], ident[0:T, 0:T])
            last.then_inc(A["ot"], 1)

        def pe_attn0_out(pe, n):
            wait(pe, A["ol"], n + 1)
            if not (isinstance(n, int) and n == B - 1):
                wait(pe, A["ptsb"], HG * (n + 1) + 4)
            for k in range(KC):
                last = mm3(pe, PS[0:T, 5, :], OH[:, k, :], OL[:, k, :], woh[:, k, :], wol[:, k, :], k == 0, k == KC - 1)
            last.then_inc(A["op"], 1)

        def pe_fold_m(pe, i, j):
            if i < NFX:
                pe.wait_ge(C["fq0"], 16 * NFX)
            elif i < NP1 - 1:
                pe.wait_ge(C["fq1"], 16 * (NP1 - 1 - NFX))
            else:
                pe.wait_ge(C["fq0"], 16 * (NFX + 1))
            wait(pe, C["msb"], i - 1)
            for h in range(2):
                for c in range(LK):
                    last = pe.matmul(PS[:, j, h * R1:(h + 1) * R1], FQR[i][:, h, c * DK:(c + 1) * DK],
                                     FQR[i][:, h, CQ + c * R1:CQ + (c + 1) * R1], start=(c == 0), stop=(c == LK - 1))
            last.then_inc(C["m"], 1)

        def pe_fold_n(pe, i, j):
            wait(pe, C["msb"], i + 1)
            wait(pe, C["nfl"], i - 1)
            at = CQ + LK * R1
            for k in range(KC):
                for h in range(2):
                    last = pe.matmul(PS[:, 2 + j, k * 128 + h * R1:k * 128 + (h + 1) * R1],
                                     FQR[i][:, h, at + k * 128:at + (k + 1) * 128], m_sb[j][:, h, :], start=True, stop=True)
            last.then_inc(C["nf"], 1)

        def pe_queries(pe, q, k, n=None):
            bank = PS[:, k % 4, :]
            if n is not None and k < 4:
                wait(pe, C["exp"], RT * n + earlier(k, 4) + RT + 1)
            elif k >= 4:
                wait(pe, C["prl"], 12 * q + k - 3)
            if k < 4:
                for m in (2 * k, 2 * k + 1):
                    for c in range(KC):
                        if isinstance(q, int):
                            xh, xl = (t[:, c, q * 2 * T:(q + 1) * 2 * T] for t in (XHC, XLC))
                        else:
                            xh, xl = (t[:, c, bass.ds(q * (2 * T), 2 * T)] for t in (XHC, XLC))
                        last = mm3(pe, bank[:, m % 2 * 2 * T:(m % 2 + 1) * 2 * T], NFH[:, c, m * 128:(m + 1) * 128],
                                   NFL[:, c, m * 128:(m + 1) * 128], xh, xl, c == 0, c == KC - 1)
            else:
                c = k - 4
                wait(pe, C["prl"], 12 * q + c // 2 + 1)
                r = slice(c % 2 * R1, (c % 2 + 1) * R1)
                for h in range(2):
                    m = c // 2 * 2 + h
                    last = mm3(pe, bank[:, h * 2 * T:(h + 1) * 2 * T], WKH[r, m, :], WKL[r, m, :], QRH[r, m, :], QRL[r, m, :],
                               True, True)
            last.then_inc(C["pr"], 1)

        def pe_keys(pe, n, j):
            wait(pe, C["kvr"], n + 1)
            wait(pe, C["ptl"], RT * (n - 1) + KVAT - LAG - 2)
            for c in range(LK):
                last = pe.transpose(PS[:, KBANK, c * 128:(c + 1) * 128], kvr[:, c, :], ident[:, :])
            last.then_inc(C["ktp"], 1)

        def pe_steps(pe, kind, n, j, q=None):
            for what, dn, t in attention_steps(kind):
                m, jj = (n, j) if dn == 0 else (n + dn, 1 - j)
                r = tile_rows(t)
                if what == "S":
                    wait(pe, C["exp"], RT * m + earlier(t, 4) + 1)
                    if t < 4:
                        wait(pe, C["prl"], 6 * m + 12 - 6 * jj)
                        wait(pe, C["ktl"], m + 1)
                    c = slice(t * 128, t * 128 + r)
                    mm3(pe, PS[0:r, t % 4, 0:NKE], QH[:, jj, c], QL[:, jj, c], KTH[jj][:, :], KTL[jj][:, :], True, True) \
                        .then_inc(C["s"], 1)
                elif what == "PT":
                    wait(pe, C["nrm"], RT * m + t + 1)
                    wait(pe, C["ptl"], RT * m + earlier(t, 3) + 1)
                    if dn == 0 and t == KVAT - LAG and kind != "last":
                        wait(pe, C["ktl"], m + 2)
                    for c in range(LK):
                        last = pe.transpose(PS[:, 4 + t % 3, c * 128:(c + 1) * 128], P1[t % 8][:, c * 128:(c + 1) * 128],
                                            ident[:, :])
                    last.then_inc(C["pt"], 1)
                elif what == "PV":
                    g, c = divmod(t, LK)
                    cols = min(512, ROWS - g * 512)
                    if c == 0:
                        wait(pe, C["ptl"], RT * m + min(4 * g + 4, RT))
                        wait(pe, C["ctxo"], NG * m + g)
                        wait(pe, C["knl"], m + 1)
                    last = mm3(pe, PS[:, 7, 0:cols], KNH[jj][:, c, :], KNL[jj][:, c, :],
                               PTH[pt_buffer(g, jj)][:, c, 0:cols], PTL[pt_buffer(g, jj)][:, c, 0:cols], c == 0, c == LK - 1)
                    if c == LK - 1:
                        last.then_inc(C["pv"], 1)
                elif what == "KV":
                    pe_keys(pe, n + 1, 1 - j)
                else:
                    pe_queries(pe, q, t, n)

        @block.tensor
        def _(pe):
            pe.wait_ge(A["consts"], 32)
            for b in range(B + 2):
                if b < B:
                    ln_transposes(pe, 0, b)
                if b >= 2:
                    v = b - 2
                    if v == 0:
                        pe.wait_ge(A["wlo"], 2)
                    wait(pe, A["vsb"], v - 1)
                    mm3(pe, PS[0:T, v % 2, :], cxh[:, v, :], cxl[:, v, :], wkvh[:, D:2 * D], wkvl[:, D:2 * D],
                        True, True).then_inc(A["vps"], 1)
            pe.wait_ge(A["wlo2"], 1)
            pe.wait_ge(LN["lo"], B)
            pe.wait_ge(A["cast"], 2)
            pe_attn0_qk(pe, 0)
            pe.wait_ge(A["vsb"], B)
            pe_attn0_scores(pe, 0, 0)

            def batch(n, j, queries=None):
                first, last = isinstance(n, int) and n == 0, isinstance(n, int) and n == B - 1
                if first:
                    pe_attn0_scores(pe, n + 1, 1 - j)
                pe_attn0_pt(pe, n, j)
                if not last and not first:
                    pe_attn0_scores(pe, n + 1, 1 - j)
                if not first:
                    pe_attn0_ot(pe, n - 1)
                if queries is not None:
                    pe_attn0_qk(pe, queries)
                pe_attn0_pv(pe, n, j)
                if not first:
                    pe_attn0_out(pe, n - 1)

            batch(0, 0, 1)
            pe.wait_ge(A["wlo2"], 2)
            with pe.Fori(0, B // 2 - 2) as p:
                batch(2 * p + 1, 1)
                batch(2 * p + 2, 0, p + 2)
            for n in range(B - 3, B):
                batch(n, n % 2)
            pe_attn0_ot(pe, B - 1)
            pe_attn0_out(pe, B - 1)
            for b in range(B + 1):
                if b < B:
                    ln_transposes(pe, 1, b)
                if b > 0:
                    pe.wait_ge(LN["lo"], B + b)
                    if b == 1:
                        pe.wait_ge(E["wglo"], 1)
                    t = slice((b - 1) * T, b * T)
                    for k in range(KC):
                        last = mm3(pe, PS[0:T, 6, (b - 1) * NE:b * NE], XHB[:, k, t], XLB[:, k, t], wg[1][:, k], wg[2][:, k],
                                   k == 0, k == KC - 1)
                    last.then_inc(E["gate"], 1)
            pe.wait_ge(E["logits"], 1)
            pe_gu(pe, 0, 0, 0)
            with pe.Fori(0, NE // 2 - 1) as i:
                pe_gu(pe, 2 * i, 1, 0)
                pe_y(pe, 2 * i, 0, 0)
                pe_gu(pe, 2 * i + 1, 0, 1)
                pe_y(pe, 2 * i, 1, 0)
                pe_gu(pe, 2 * i + 1, 1, 1)
                pe_y(pe, 2 * i + 1, 0, 1)
                pe_gu(pe, 2 * i + 2, 0, 0)
                pe_y(pe, 2 * i + 1, 1, 1)
            pe_gu(pe, NE - 2, 1, 0)
            pe_y(pe, NE - 2, 0, 0)
            pe_gu(pe, NE - 1, 0, 1)
            pe_y(pe, NE - 2, 1, 0)
            pe_gu(pe, NE - 1, 1, 1)
            pe_y(pe, NE - 1, 0, 1)
            pe_y(pe, NE - 1, 1, 1)
            pe_fold_m(pe, 0, 0)
            for i in range(NP1):
                if i + 1 < NP1:
                    pe_fold_m(pe, i + 1, (i + 1) % 2)
                pe_fold_n(pe, i, i % 2)
            for b in range(B):
                ln_transposes(pe, 2, b)
            pe.wait_ge(LN["lo"], 3 * B)
            pe_keys(pe, 0, 0)
            pe.wait_ge(C["nfl"], NP1)
            pe.wait_ge(C["krl"], 1)
            for k in range(12):
                pe_queries(pe, 0, k)
            pe_steps(pe, "even", 0, 0)
            with pe.Fori(0, B // 2 - 1) as p:
                pe_steps(pe, "odd", 2 * p + 1, 1, p + 1)
                pe_steps(pe, "even", 2 * p + 2, 0)
            pe_steps(pe, "last", B - 1, 1)
            for h in range(NH0):
                i, j = h // 2, h // 2 % 4
                if h % 2 == 0:
                    pe.wait_ge(O[f"fp{j}"], 16 * (i // 4 + 1))
                wait(pe, O["pfl"], h - 3)
                pe.matmul(PS[:, h % 4, :], FPR[j][:, h % 2, 0:DK], FPR[j][:, h % 2, DK:FP], start=True, stop=True) \
                    .then_inc(O["pf"], 1)

            def project(n, j):
                wait(pe, O["cxl"], n + 1)
                wait(pe, O["res"], n - 1)
                for h in range(NH0):
                    t = slice(h * T, (h + 1) * T)
                    last = mm3(pe, PS[0:T, 4 + j, :], CXH[j][:, t], CXL[j][:, t], PFH[:, h, :], PFL[:, h, :], h == 0, h == NH0 - 1)
                last.then_inc(O["out"], 1)

            pe.wait_ge(O["pfl"], NH0)
            def pe_weights(n, odd, p=None):
                for i, (kind, _) in enumerate(wtiles(n if p is None else (p,), odd)):
                    wait(pe, W["sub"], 3 * n + i + 1)
                    wait(pe, W["ev"], 3 * (n - 1) + i + 1)
                    ch = KC if kind == "up" else IC
                    for c in range(ch):
                        last = pe.transpose(wbank(i, ch)[:, c, :], WQT[i][:, c * 128:(c + 1) * 128], identb[:, :])
                    last.then_inc(W["tr"], 1)
                    wait(pe, W["dg"], 3 * n + i + 1)
                    wait(pe, W["sb"], 3 * (n - 2) + 3)
                    pe.matmul(PS[0:T, 6 + odd, i * 128:(i + 1) * 128], ones[:, :], diag[i][:, :], start=True, stop=True) \
                        .then_inc(W["bc"], 1)

            pe.wait_ge(W["ones"], 1)
            with pe.Fori(0, B // 2) as p:
                project(2 * p, 0)
                pe_weights(2 * p, 0, p)
                project(2 * p + 1, 1)
                pe_weights(2 * p + 1, 1, p)
            pe_weights(B, 0)

            def pe_xq(m, j):
                wait(pe, F["sub"], m + 1)
                if isinstance(m, int) and m == 0:
                    pe.wait_ge(W["sb"], UT + DT)
                wait(pe, F["xev"], m)
                for k in range(KC):
                    last = pe.transpose(PS[:, 6, :].bitcast(BF16)[:, k * T:(k + 1) * T], XQ[j][:, k * 128:(k + 1) * 128],
                                        identb[0:T, 0:T])
                last.then_inc(F["xt"], 1)

            def pe_gate_up(m, j, c):
                if c == 0:
                    wait(pe, F["xev"], m + 1)
                for which, free, done in ((0, "gs", "gps"), (1, "us", "ups")):
                    wait(pe, F[free], GC * m + c - 1)
                    at = which * FI + c * GW_
                    for k in range(KC):
                        last = pe.matmul(PS[0:T, 2 * which + c % 2, 0:GW_], XQT[j][:, k, :], W1Q[:, k, at:at + GW_],
                                         start=(k == 0), stop=(k == KC - 1))
                    last.then_inc(F[done], 1)

            def pe_ht(n, j):
                wait(pe, F["hsub"], n + 1)
                for g, (a, z) in enumerate(HTG):
                    wait(pe, F["hev"], 2 * (n - 1) + g + 1)
                    for c in range(a, z):
                        last = pe.transpose(PS[:, 4 + g, :].bitcast(BF16)[:, (c - a) * T:(c - a + 1) * T],
                                            HQ[j][:, c * 128:(c + 1) * 128], identb[0:T, 0:T])
                    last.then_inc(F["ht"], 1)

            def pe_down(n, j):
                wait(pe, F["hev"], 2 * n + 2)
                wait(pe, F["y"], n)
                for c in range(IC):
                    last = pe.matmul(PS[0:T, 7, :], HQT[j][:, c, :], W2Q[:, c, :], start=(c == 0), stop=(c == IC - 1))
                last.then_inc(F["dn"], 1)

            def pe_ffn(n, j, more=True):
                for c in range(GC - 1):
                    pe_gate_up(n + 1, 1 - j, c)
                pe_ht(n, j)
                pe_gate_up(n + 1, 1 - j, GC - 1)
                if more:
                    pe_xq(n + 2, j)
                pe_down(n, j)

            pe_xq(0, 0)
            pe.wait_ge(W["ev"], UT + DT)
            for c in range(GC):
                pe_gate_up(0, 0, c)
                if c == 1:
                    pe_xq(1, 1)
            with pe.Fori(0, B // 2 - 1) as p:
                pe_ffn(2 * p, 0)
                pe_ffn(2 * p + 1, 1)
            pe_ffn(B - 2, 0, False)
            pe_ht(B - 1, 1)
            pe_down(B - 1, 1)

        def dve_gu(dve, e, half):
            for c in range(NCH):
                step, par = NCH * (2 * e + half) + c, (half + c) % 2
                r = slice(0, FC[c])
                wait(dve, E["ups"], step + 1)
                wait(dve, E["silu"], step + 1)
                wait(dve, E["hlo"], step - 1)
                dve.tensor_tensor(h32[r, par, :], silu[r, par, :], PS[r, 2 + par, 0:HALF], ALU.mult).then_inc(E["hmul"], 1)
                if c > 0:
                    dve_hlow(dve, e, half, c - 1)
            dve_hlow(dve, e, half, NCH - 1)

        def dve_hlow(dve, e, half, c):
            step, par = NCH * (2 * e + half) + c, (half + c) % 2
            r, t = slice(0, FC[c]), slice(half * HALF, (half + 1) * HALF)
            wait(dve, E["hhi"], step + 1)
            dve.tensor_tensor(HL[r, c, t], h32[r, par, :], HH[r, c, t].bitcast(F32), ALU.subtract).then_inc(E["hlo"], 1)

        def dve_y(dve, e, half, last=False):
            u = 2 * e + half
            for q in range(B // 2):
                b = half * 4 + q
                wait(dve, E["yps"], B // 2 * u + q + 1)
                wait(dve, E["yacc"], B // 2 * (u - 2) + q + 1)
                w = GW[:, e, b:b + 1] if isinstance(e, int) else GW[:, bass.ds(e, 1), b]
                dve.scalar_tensor_tensor(X[:, b, :], PS[0:T, 4 + q, :], w, X[:, b, :], ALU.mult, ALU.add) \
                    .then_inc(E["yacc"], 1)
                if last:
                    dve.wait_ge(E["yacc"], B * e + b + 1)
                    lnc_batch(dve, b)

        def dve_hi12(dve, e, j):
            wait(dve, E["d12"], 16 * (e + 1))
            wait(dve, E["ups"], NCH * 2 * (e - 1))
            dve.tensor_copy(wh[j][:, 0:W12], wraw[:, 0:W12]).then_inc(E["hi12"], 1)

        def dve_hi3(dve, e, j):
            wait(dve, E["d3"], 32 * (e + 1))
            wait(dve, E["yps"], B * (e - 1))
            dve.tensor_copy(wh[j][:, W12:], wraw[:, W12:]).then_inc(E["hi3"], 1)

        def dve_gating(dve):
            dve.wait_ge(E["gate"], B)
            dve.tensor_copy(logits[:, :, :], PS[0:T, 6, 0:B * NE].rearrange("p (b e) -> p b e", b=B)).then_inc(E["logits"], 1)
            dve.wait_ge(E["logits"], 1)
            for b in range(B):
                dve.max(top8[:, b, :], logits[:, b, :]).then_inc(E["gating"], 1)
            dve.wait_ge(E["gating"], 8)
            for b in range(B):
                dve.max_index(top8i[:, b, :], top8[:, b, :], logits[:, b, :]).then_inc(E["gating"], 1)
            dve.tensor_tensor(gd[:, 0, :], top8[:, :, 1], top8[:, :, 0], ALU.subtract).then_inc(E["diff"], 1)
            dve.wait_ge(E["gating"], 16)
            dve.tensor_copy(top2i[:, :, :], top8i[:, :, 0:2]).then_inc(E["gating"], 1)
            dve.wait_ge(E["ex"], 1)
            dve.tensor_scalar(gd[:, 2, :], gd[:, 1, :], 1.0, None, ALU.add).then_inc(E["gating"], 1)
            dve.wait_ge(E["gating"], 18)
            dve.reciprocal(gd[:, 3, :], gd[:, 2, :]).then_inc(E["gating"], 1)
            dve.wait_ge(E["gating"], 19)
            dve.tensor_tensor(gd[:, 2, :], gd[:, 3, :], gd[:, 1, :], ALU.mult).then_inc(E["gating"], 1)
            dve.wait_ge(E["gating"], 17)
            dve.wait_ge(E["consts"], 32)
            for i in range(2):
                dve.tensor_tensor(geq[:, i, :, :], iota[:, None, :].broadcast_to((T, B, NE)),
                                  top2i[:, :, i, None].broadcast_to((T, B, NE)), ALU.is_equal).then_inc(E["gating"], 1)
            dve.wait_ge(E["gating"], 22)
            dve.wait_ge(E["gating"], 20)
            for i in range(2):
                dve.tensor_tensor(geq[:, 2 + i, :, :], geq[:, i, :, :],
                                  gd[:, 3 - i, :, None].broadcast_to((T, B, NE)), ALU.mult).then_inc(E["gating"], 1)
            dve.wait_ge(E["gating"], 24)
            dve.tensor_tensor(GW[:, :, :].rearrange("p e b -> p b e"), geq[:, 2, :, :], geq[:, 3, :, :], ALU.add) \
                .then_inc(E["gating"], 1)
            dve.wait_ge(E["gating"], 25)

        def dve_attn0_softmax(dve, n, j):
            wait(dve, A["pt"], HG * (n - 1))
            for i in range(HG):
                wait(dve, A["sc"], HG * n + i + 1)
                dve.tensor_reduce(mx0[:, j, i, :], S0[i], AX.X, ALU.max).then_inc(A["mx"], 1)
            for i in range(HG):
                wait(dve, A["mx"], HG * n + i + 1)
                dve.tensor_tensor(P0[j][:, i, :, :], S0[i], mx0[:, j, i, :, None].broadcast_to((T, MT0, T)),
                                  ALU.subtract).then_inc(A["sub"], 1)

        def dve_attn0_k(dve, p):
            for m in range(MT0):
                wait(dve, A["qk"], 2 * MT0 * p + 2 * m + 2)
                if m == 0:
                    wait(dve, A["sc"], 2 * HG * p)
                dve.tensor_copy(KT[:, m, :, :], PS[:, 7, 0:2 * T].rearrange("p (b t) -> p b t", b=2)).then_inc(A["ksb"], 1)

        def dve_attn0_norm(dve, n):
            ov = O0[:, :].rearrange("p (m i d) -> p i m d", m=MT0, i=HG)
            for g in range(2):
                wait(dve, A["pv"], 2 * n + g + 1)
                dve.reciprocal(rs0[:, 2 * g:2 * g + 2, :], OV[g][:, :, :, HD0]).then_inc(A["rs"], 1)
                wait(dve, A["rs"], 2 * n + g + 1)
                if g == 0:
                    wait(dve, A["ot"], n)
                for i in range(2):
                    x_ = dve.tensor_tensor(ov[:, 2 * g + i, :, :], OV[g][:, i, :, 0:HD0],
                                      rs0[:, 2 * g + i, :, None].broadcast_to((T, MT0, HD0)), ALU.mult)
                x_.then_inc(A["onorm"], 1)

        def dve_attn0_low(dve, n):
            wait(dve, A["oh"], n + 1)
            dve.tensor_tensor(OL[:, :, :], TP[0], OH[:, :, :].bitcast(F32), ALU.subtract).then_inc(A["ol"], 1)

        def dve_attn0_add(dve, n):
            wait(dve, A["op"], n + 1)
            dve.tensor_tensor(one(X, n), one(X, n), PS[0:T, 5, :], ALU.add).then_inc(A["res"], 1)
            dve.wait_ge(A["res"], n + 1)
            lne_batch(dve, n)

        def dve_fold(dve, i, j):
            wait(dve, C["nfh"], i + 1)
            dve.tensor_tensor(fold_cols(NFL, i), PS[:, 2 + j, :].rearrange("p (k n) -> p k n", k=KC),
                              fold_cols(NFH, i).bitcast(F32), ALU.subtract).then_inc(C["nfl"], 1)

        def dve_queries(dve, q, k):
            wait(dve, C["prh"], 12 * q + k + 1)
            o, bank = queries_part(k, False)
            hi, _ = queries_part(k, True)
            dve.tensor_tensor(o, bank, hi.bitcast(F32), ALU.subtract).then_inc(C["prl"], 1)

        def dve_keys(dve, n, j):
            wait(dve, C["kth"], n + 1)
            dve.tensor_tensor(KTL[j][:, :], PS[:, KBANK, 0:NKE], KTH[j][:, :].bitcast(F32), ALU.subtract).then_inc(C["ktl"], 1)

        def dve_steps(dve, kind, n, j, q=None):
            behind = []

            def invert(m, jj, t):
                r = slice(0, tile_rows(t))
                wait(dve, C["exp"], RT * m + t + 1)
                dve.reciprocal(rinv[r, jj, t:t + 1], rsum[r, jj, t:t + 1]).then_inc(C["inv"], 1)

            for what, dn, t in attention_steps(kind, vector=True):
                m, jj = (n, j) if dn == 0 else (n + dn, 1 - j)
                if what == "S":
                    r = slice(0, tile_rows(t))
                    wait(dve, C["s"], RT * m + t + 1)
                    dve.tensor_reduce(nmx[r, jj, t:t + 1], PS[r, t % 4, 0:NK], AX.X, ALU.max, negate=True).then_inc(C["max"], 1)
                elif what == "PT":
                    wait(dve, C["pth"], RT * m + t + 1)
                    dve.tensor_tensor(pt_place(PTL, t, jj), turned(t), pt_place(PTH, t, jj).bitcast(F32), ALU.subtract) \
                        .then_inc(C["ptl"], 1)
                elif what == "PV":
                    continue
                elif what == "KV":
                    dve_keys(dve, n + 1, 1 - j)
                elif what == "PR":
                    dve_queries(dve, q, t)
                if behind and (what in ("S", "PR") or behind[0][2] == RT - 1 and kind == "last"):
                    invert(*behind.pop(0))
                if what == "S":
                    behind.append((m, jj, t))
            for rest in behind:
                invert(*rest)

        @block.vector
        def _(dve):
            for b in range(B):
                if b % (B // 2) == 0:
                    dve.wait_ge(A["x" if b == 0 else "x2"], 16)
                ln_batch(dve, b)
            ln_vec(dve)

            def split(k):
                a, z, _ = SPLITS[k]
                dve.wait_ge(A["whi"], k + 1)
                dve.tensor_tensor(lo0[:, a:z], raw0[:, a:z], hi0[:, a:z].bitcast(F32), ALU.subtract).then_inc(A["wlo"], 1)

            normalise(dve, 0, 0)
            normalise(dve, 0, 1)
            split(0)
            split(1)
            for b in range(B):
                ln_low(dve, 0, b, XH, XL)
                if b + 2 < B:
                    normalise(dve, 0, b + 2)
            dve_attn0_k(dve, 0)
            dve_attn0_softmax(dve, 0, 0)

            def batch(n, j, queries=None):
                first, last = isinstance(n, int) and n == 0, isinstance(n, int) and n == B - 1
                if not last:
                    dve_attn0_softmax(dve, n + 1, 1 - j)
                if not first:
                    dve_attn0_low(dve, n - 1)
                if queries is not None:
                    dve_attn0_k(dve, queries)
                dve_attn0_norm(dve, n)
                if not first:
                    dve_attn0_add(dve, n - 1)

            batch(0, 0, 1)
            with dve.Fori(0, B // 2 - 2) as p:
                batch(2 * p + 1, 1)
                batch(2 * p + 2, 0, p + 2)
            for n in range(B - 3, B):
                batch(n, n % 2)
            dve_attn0_low(dve, B - 1)
            dve_attn0_add(dve, B - 1)
            lne_vec(dve)
            normalise(dve, 1, 0)
            normalise(dve, 1, 1)
            dve.wait_ge(E["wghi"], 1)
            dve.tensor_tensor(wg[2][:, :, :], wg[0][:, :, :], wg[1][:, :, :].bitcast(F32), ALU.subtract).then_inc(E["wglo"], 1)
            dve_hi12(dve, 0, 0)
            for b in range(B):
                ln_low(dve, 1, b, XHB, XLB)
                if b == 3:
                    dve_hi3(dve, 0, 0)
                if b + 2 < B:
                    normalise(dve, 1, b + 2)
            dve_gating(dve)
            dve_gu(dve, 0, 0)
            with dve.Fori(0, NE // 2 - 1) as i:
                dve_hi12(dve, 2 * i + 1, 1)
                dve_gu(dve, 2 * i, 1)
                dve_y(dve, 2 * i, 0)
                dve_hi3(dve, 2 * i + 1, 1)
                dve_gu(dve, 2 * i + 1, 0)
                dve_y(dve, 2 * i, 1)
                dve_hi12(dve, 2 * i + 2, 0)
                dve_gu(dve, 2 * i + 1, 1)
                dve_y(dve, 2 * i + 1, 0)
                dve_hi3(dve, 2 * i + 2, 0)
                dve_gu(dve, 2 * i + 2, 0)
                dve_y(dve, 2 * i + 1, 1)
            dve_hi12(dve, NE - 1, 1)
            dve_gu(dve, NE - 2, 1)
            dve_y(dve, NE - 2, 0)
            dve_hi3(dve, NE - 1, 1)
            dve_gu(dve, NE - 1, 0)
            dve_y(dve, NE - 2, 1)
            dve_gu(dve, NE - 1, 1)
            dve_y(dve, NE - 1, 0, True)
            dve_y(dve, NE - 1, 1, True)
            lnc_vec(dve)
            normalise(dve, 2, 0)
            normalise(dve, 2, 1)
            dve.wait_ge(C["krh"], 1)
            dve.tensor_tensor(WKL[:, :, :], kr_raw[:, :, :], WKH[:, :, :].bitcast(F32), ALU.subtract).then_inc(C["krl"], 1)
            with dve.Fori(0, NP1 // 2) as i:
                dve_fold(dve, 2 * i, 0)
                dve_fold(dve, 2 * i + 1, 1)
            for b in range(B):
                ln_low(dve, 2, b, XHC, XLC)
                if b + 2 < B:
                    normalise(dve, 2, b + 2)
            dve_keys(dve, 0, 0)
            for k in range(12):
                dve_queries(dve, 0, k)
            dve_steps(dve, "even", 0, 0)
            with dve.Fori(0, B // 2 - 1) as p:
                dve_steps(dve, "odd", 2 * p + 1, 1, p + 1)
                dve_steps(dve, "even", 2 * p + 2, 0)
            dve_steps(dve, "last", B - 1, 1)
            def low_ctx(n, j):
                wait(dve, O["cxh"], n + 1)
                dve.tensor_tensor(CXL[j][:, :], CXR[j][:, :], CXH[j][:, :].bitcast(F32), ALU.subtract).then_inc(O["cxl"], 1)

            for h in range(NH0):
                dve.wait_ge(O["pfh"], h + 1)
                dve.tensor_tensor(PFL[:, h, :], PS[:, h % 4, :], PFH[:, h, :].bitcast(F32), ALU.subtract).then_inc(O["pfl"], 1)
                if h == NH0 - 3:
                    low_ctx(0, 0)

            def add_out(n, j):
                wait(dve, O["out"], n + 1)
                xs = X[:, n, :] if isinstance(n, int) else X[:, bass.ds(n, 1), :].rearrange("p a d -> p (a d)")
                dve.tensor_tensor(xs, xs, PS[0:T, 4 + j, :], ALU.add).then_inc(O["res"], 1)
                dve.wait_ge(O["res"], n + 1)
                lnf_batch(dve, n)

            def dve_weights(n, odd, p=None):
                tiles = wtiles(n if p is None else (p,), odd)

                def quantise(i, kind):
                    wait(dve, W["mag"], 3 * n + i + 1)
                    wait(dve, W["tr"], 3 * (n - 1) + i + 1)
                    w = D if kind == "up" else FI
                    dve.tensor_scalar(WQT[i][:, 0:w], WRT[i][:, 0:w], MAGIC, None, ALU.subtract).then_inc(W["sub"], 1)

                for i, (kind, _) in enumerate(tiles):
                    w = D if kind == "up" else FI
                    wait(dve, W[f"ld{i}"], 16 * n + 16)
                    wait(dve, W["dg"], 3 * (n - 1) + i + 1)
                    dve.tensor_reduce(wsc[i][:, 0:1], WRT[i][:, 0:w], AX.X, ALU.max, apply_absolute_value=True).then_inc(W["max"], 1)
                    wait(dve, W["max"], 3 * n + i + 1)
                    dve.tensor_scalar(wsc[i][:, 1:2], wsc[i][:, 0:1], 1.0 / QMAX, QEPS, ALU.mult, ALU.max).then_inc(W["sc"], 1)
                    wait(dve, W["sc"], 3 * n + i + 1)
                    dve.reciprocal(wsc[i][:, 2:3], wsc[i][:, 1:2]).then_inc(W["inv"], 1)
                    if i > 0:
                        quantise(i - 1, tiles[i - 1][0])
                quantise(len(tiles) - 1, tiles[-1][0])

            def dve_scales(n, odd, p=None):
                tiles = wtiles(n if p is None else (p,), odd)
                wait(dve, W["bc"], 3 * n + len(tiles))
                ups = sum(kind == "up" for kind, _ in tiles)
                first = tiles[0][1] * 128
                o = S1B[:, first:first + ups * 128] if isinstance(first, int) else S1B[:, bass.ds(first, ups * 128)]
                dve.tensor_copy(o, PS[0:T, 6 + odd, 0:ups * 128]).then_inc(W["sb"], ups)
                if ups < len(tiles):
                    dve.tensor_copy(S2B[:, cols_at(tiles[-1][1], 128)], PS[0:T, 6 + odd, ups * 128:(ups + 1) * 128])                         .then_inc(W["sb"], 1)

            with dve.Fori(0, B // 2 - 1) as p:
                low_ctx(2 * p + 1, 1)
                dve_weights(2 * p, 0, p)
                add_out(2 * p, 0)
                dve_scales(2 * p, 0, p)
                low_ctx(2 * p + 2, 0)
                dve_weights(2 * p + 1, 1, p)
                add_out(2 * p + 1, 1)
                dve_scales(2 * p + 1, 1, p)
            low_ctx(B - 1, 1)
            dve_weights(B - 2, 0)
            add_out(B - 2, 0)
            dve_scales(B - 2, 0)
            dve_weights(B - 1, 1)
            add_out(B - 1, 1)
            dve_scales(B - 1, 1)
            lnf_vec(dve)
            dve_weights(B, 0)
            dve_scales(B, 0)


            def dve_xq(m, j):
                xs = X[:, m, :] if isinstance(m, int) else X[:, bass.ds(m, 1), :].rearrange("p a d -> p (a d)")
                mean = mv[:, m, 0:1] if isinstance(m, int) else mv[:, bass.ds(m, 1), 0]
                r = rstd[:, m:m + 1] if isinstance(m, int) else rstd[:, bass.ds(m, 1)]
                wait(dve, F["mag"], m - 1)
                dve.tensor_scalar(xn[:, j, :], xs, mean, r, ALU.subtract, ALU.mult).then_inc(F["xn"], 1)
                wait(dve, F["xn"], m + 1)
                dve.tensor_reduce(sx[:, j, 0:1], xn[:, j, :], AX.X, ALU.max, apply_absolute_value=True).then_inc(F["xscale"], 1)
                wait(dve, F["xscale"], 2 * m + 1)
                dve.tensor_scalar(sx[:, j, 1:2], sx[:, j, 0:1], 1.0 / QMAX, QEPS, ALU.mult, ALU.max).then_inc(F["xscale"], 1)
                wait(dve, F["xscale"], 2 * m + 2)
                dve.reciprocal(sx[:, j, 2:3], sx[:, j, 1:2]).then_inc(F["inv"], 1)

            def dve_xsub(m, j):
                wait(dve, F["mag"], m + 1)
                wait(dve, F["xt"], m - 1)
                dve.tensor_scalar(XQ[j][:, :], XM[j][:, :], MAGIC, None, ALU.subtract).then_inc(F["sub"], 1)

            def dve_gate_up(m, j, c):
                at = c * GW_
                wait(dve, F["gps"], GC * m + c + 1)
                wait(dve, F["silu"], GC * m + c - 1)
                dve.scalar_tensor_tensor(GS[c % 2][:, :], PS[0:T, c % 2, 0:GW_], sx[:, j, 1:2], S1B[:, at:at + GW_],
                                         ALU.mult, ALU.mult).then_inc(F["gs"], 1)
                wait(dve, F["ups"], GC * m + c + 1)
                wait(dve, F["h"], GC * m + c - 1)
                dve.scalar_tensor_tensor(US[c % 2][:, :], PS[0:T, 2 + c % 2, 0:GW_], sx[:, j, 1:2], S1B[:, FI + at:FI + at + GW_],
                                         ALU.mult, ALU.mult).then_inc(F["us"], 1)

            def dve_hmax(n, j, c):
                wait(dve, F["h"], GC * n + c + 1)
                dve.tensor_reduce(hmx[:, j, c:c + 1], H1[j][:, c * GW_:(c + 1) * GW_], AX.X, ALU.max,
                                  apply_absolute_value=True).then_inc(F["hmax"], 1)

            def dve_hscale(n, j):
                wait(dve, F["hmax"], GC * (n + 1))
                dve.tensor_reduce(sh[:, j, 0:1], hmx[:, j, :], AX.X, ALU.max).then_inc(F["hscale"], 1)
                wait(dve, F["hscale"], 2 * n + 1)
                dve.tensor_scalar(sh[:, j, 1:2], sh[:, j, 0:1], 1.0 / QMAX, QEPS, ALU.mult, ALU.max).then_inc(F["hscale"], 1)
                wait(dve, F["hscale"], 2 * n + 2)
                dve.reciprocal(sh[:, j, 2:3], sh[:, j, 1:2]).then_inc(F["hinv"], 1)

            def dve_hsub(n, j):
                wait(dve, F["hmag"], n + 1)
                wait(dve, F["ht"], 2 * (n - 1))
                dve.tensor_scalar(HQ[j][:, :], H1[j][:, :], MAGIC, None, ALU.subtract).then_inc(F["hsub"], 1)

            def dve_out(n, j):
                wait(dve, F["dn"], n + 1)
                wait(dve, F["res"], n - 1)
                dve.scalar_tensor_tensor(Y2[j][:, :], PS[0:T, 7, :], sh[:, j, 1:2], S2B[:, :],
                                         ALU.mult, ALU.mult).then_inc(F["y"], 1)

            def dve_ffn(n, j, more=True):
                dve_gate_up(n + 1, 1 - j, 0)
                dve_hmax(n, j, 3)
                dve_hscale(n, j)
                dve_gate_up(n + 1, 1 - j, 1)
                if more:
                    dve_xq(n + 2, j)
                dve_hsub(n, j)
                dve_hmax(n + 1, 1 - j, 0)
                dve_gate_up(n + 1, 1 - j, 2)
                dve_hmax(n + 1, 1 - j, 1)
                if more:
                    dve_xsub(n + 2, j)
                dve_gate_up(n + 1, 1 - j, 3)
                dve_hmax(n + 1, 1 - j, 2)
                dve_out(n, j)

            dve_xq(0, 0)
            dve_xsub(0, 0)
            dve_xq(1, 1)
            dve_xsub(1, 1)
            for c in range(GC):
                dve_gate_up(0, 0, c)
                if c > 0:
                    dve_hmax(0, 0, c - 1)
            with dve.Fori(0, B // 2 - 1) as p:
                dve_ffn(2 * p, 0)
                dve_ffn(2 * p + 1, 1)
            dve_ffn(B - 2, 0, False)
            dve_hmax(B - 1, 1, GC - 1)
            dve_hscale(B - 1, 1)
            dve_hsub(B - 1, 1)
            dve_out(B - 1, 1)


def rope_tables():
    f = np.float32
    inv = (f(1.0) / f(10000.0) ** (np.arange(0, DK, 2, dtype=f) / f(DK))).astype(f)
    angle = (np.arange(NK, dtype=f)[:, None] * inv[None, :]).astype(f)
    cos, sin = (np.repeat(fn(angle), 2, axis=-1).astype(f) for fn in (np.cos, np.sin))
    sin[:, :DK // 2] *= -1

    def lay(t):
        rows = np.zeros((LK * 128, DK), f)
        rows[:NK] = t
        return rows.reshape(LK, 128, DK).transpose(1, 0, 2)

    return lay(cos), lay(sin)


def kernel(**inputs):
    import concourse.bacc as bacc
    from concourse.bass_utils import run_bass_kernel_spmd

    w = {n: np.asarray(a) for n, a in inputs.items()}
    f = np.float32
    ctx = w["ctx_512"]

    def columns(m):
        return m.T.reshape(KC, 128, -1).transpose(1, 0, 2).reshape(128, -1)

    def head_rows(parts):
        n = sum(p.shape[2] for p in parts)
        return np.concatenate(parts, 2).reshape(NP1, 2, 128, n).transpose(0, 2, 1, 3)

    cos, sin = rope_tables()
    up_down = np.stack([w["L0_ffn_W1"], w["L0_ffn_W2"]], 1)
    kc_q = w["L1_xattn_w_kc_q"].transpose(0, 2, 1).reshape(NH0, LK, 128, DK).transpose(0, 2, 1, 3)
    w_qr = w["L1_xattn_W_qr"].reshape(NH0, LK, 128, R1).transpose(0, 2, 1, 3)
    arrays = dict(
        x_in=w["x"],
        ctx_t_in=ctx.transpose(2, 0, 1),
        wq0_in=columns(w["L0_xattn_Wq"]),
        wkv0_in=w["L0_xattn_Wkv_expand"].T,
        wout0_in=columns(w["L0_xattn_Wout"]),
        ident_in=np.eye(128, dtype=f),
        mask_in=np.where(np.tril(np.ones((T, T), bool)), f(0), f(-1e30)).astype(f),
        wg_in=w["L0_ffn_Wg"].T.reshape(KC, 128, NE).transpose(1, 0, 2),
        w12_in=up_down.reshape(NE, 2, FH, KC, 128).transpose(0, 4, 1, 3, 2).reshape(NE, 128, W12),
        w3_in=w["L0_ffn_W3"].transpose(0, 2, 1),
        iota_in=np.tile(np.arange(NE, dtype=f), (T, 1)),
        ctxn_in=ctx,
        cos_in=cos,
        sin_in=sin,
        foldq_in=head_rows([kc_q.reshape(NH0, 128, LK * DK), w_qr.reshape(NH0, 128, LK * R1),
                            w["L1_xattn_Wq"].reshape(NH0, 128, D)]),
        krt_in=w["L1_xattn_W_kr"].transpose(0, 2, 1).reshape(NP1, 128, DK).transpose(1, 0, 2),
        foldp_in=head_rows([w["L1_xattn_w_kc_kv"], w["L1_xattn_Wo"].T.reshape(NH0, 128, D)]),
        wup_in=w["L1_ffn_w_gate_up"],
        wdown_in=w["L1_ffn_w_down"],
    )
    arrays = {n: np.ascontiguousarray(a) for n, a in arrays.items()}

    nc = bacc.Bacc("TRN2", target_bir_lowering=False, num_devices=1)
    args = [nc.dram_tensor(n, a.shape, mybir.dt.from_np(a.dtype), kind="ExternalInput").ap()
            for n, a in arrays.items()]
    args.append(nc.dram_tensor("out", (B, T, D), F32, kind="ExternalOutput").ap())
    build_kernel(nc, *args)
    r = run_bass_kernel_spmd(nc, [arrays], core_ids=[0])
    return r.results[0]["out"]
```
